# Optimizing a Trainium2 kernel written in Bass

```python
import numpy as np
import jax
import jax.numpy as jnp

def _softmax(x, axis=-1):
    return jax.nn.softmax(x, axis=axis)

def _gelu(x):
    return jax.nn.gelu(x, approximate=True)

def _silu(x):
    return jax.nn.silu(x)

def _sigmoid(x):
    return jax.nn.sigmoid(x)

def _layernorm(x, axis=-1, eps=1e-05):
    m = jnp.mean(x, axis=axis, keepdims=True)
    v = jnp.var(x, axis=axis, keepdims=True)
    return (x - m) / jnp.sqrt(v + eps)

def _scatter_add(tgt, idx, src, axis=0):
    return tgt.at[idx].add(src)

def _segment_sum(src, seg, n):
    return jax.ops.segment_sum(src, seg, n)
kernel_name = 'mk_xattn_ffn_d1_seqx_r4_7ee2a3'

def setup_inputs(seed: int=0):
    np.random.seed(seed)
    _w = jnp.asarray

    def _rec_inputs():
        import jax
        import jax.numpy as jnp
        _rk = jax.random.key(seed)
        x = -0.0002928 + 1 * jax.random.normal(jax.random.fold_in(_rk, 1), (8, 512, 256), jnp.float32)
        _lenS = 512 - jax.random.randint(jax.random.fold_in(_rk, 7), (8,), 0, max(1, 512 // 4) + 1, jnp.int32)
        _lenS2 = 64 - jax.random.randint(jax.random.fold_in(_rk, 8), (8,), 0, max(1, 64 // 4) + 1, jnp.int32)
        _ctx_1024P = jax.random.normal(jax.random.fold_in(_rk, 11), (8, 16, 256), jnp.float32)
        _ctx_1024c = jax.random.dirichlet(jax.random.fold_in(_rk, 511), 0.3 * jnp.ones((16,), jnp.float32), (8, 64))
        _ctx_1024t = jnp.einsum('bsk,bkd->bsd', _ctx_1024c, _ctx_1024P)
        _ctx_1024t = _ctx_1024t * jax.lax.rsqrt(jnp.mean(jnp.square(_ctx_1024t)) + 1e-12) * 0.953939
        ctx_1024 = -1.39393e-06 + 0.999914 * (_ctx_1024t + 0.3 * jax.random.normal(jax.random.fold_in(_rk, 611), (8, 64, 256), jnp.float32))
        _validS = jnp.arange(512)[None, :] < _lenS[:, None]
        _validS2 = jnp.arange(64)[None, :] < _lenS2[:, None]
        _causal = jnp.tril(jnp.ones((512, 512), dtype=bool))
        mask_Bx1xSxS2_ik1 = jnp.where(jnp.broadcast_to(_validS2[:, None, None, :], (8, 1, 512, 64)), 1, 0).astype(jnp.int32)
        return (x, ctx_1024, mask_Bx1xSxS2_ik1)
    x, ctx_1024, mask_Bx1xSxS2_ik1 = _rec_inputs()

    def _L0_xattn_setup():
        import jax, jax.numpy as jnp
        import numpy as np
        B, L, C, H = (2, 512, 256, 16)
        D = C // H
        key = jax.random.key(seed)
        ks = jax.random.split(key, 13)
        s = 1.0 / np.sqrt(C)
        inp = {'query': jax.random.normal(ks[0], (B, L, C), jnp.float32), 'key': jax.random.normal(ks[1], (B, L, C), jnp.float32), 'value': jax.random.normal(ks[2], (B, L, C), jnp.float32), 'mask': jax.random.randint(ks[3], (B, 1, L, L), 0, 2, jnp.int32), 'WQ': jax.random.normal(ks[4], (C, C), jnp.float32) * s, 'bQ': jnp.zeros((C,), jnp.float32), 'WK': jax.random.normal(ks[5], (C, C), jnp.float32) * s, 'bK': jnp.zeros((C,), jnp.float32), 'WV': jax.random.normal(ks[6], (C, C), jnp.float32) * s, 'bV': jnp.zeros((C,), jnp.float32), 'WO': jax.random.normal(ks[7], (C, C), jnp.float32) * s, 'bO': jnp.zeros((C,), jnp.float32)}
        return inp
    _L0_xattn_all = _L0_xattn_setup()
    _L0_xattn_in = {k: v for k, v in _L0_xattn_all.items() if k in ('WQ', 'bQ', 'WK', 'bK', 'WV', 'bV', 'WO', 'bO')}
    del _L0_xattn_all

    def _L0_ffn_setup():
        import jax, jax.numpy as jnp
        import numpy as np
        D_MODEL = 256
        HIDDEN = 1024
        N_ROUTING = 2
        key = jax.random.key(seed)
        ks = jax.random.split(key, 10)
        s = 0.02
        x = jax.random.normal(ks[0], (4, 1024, D_MODEL), dtype=jnp.float32)
        gate_w = jax.random.normal(ks[1], (N_ROUTING, D_MODEL), dtype=jnp.float32) * s
        w1 = jax.random.normal(ks[2], (N_ROUTING, D_MODEL, HIDDEN), dtype=jnp.float32) * s
        b1 = jax.random.normal(ks[3], (N_ROUTING, HIDDEN), dtype=jnp.float32) * s
        w2 = jax.random.normal(ks[4], (N_ROUTING, HIDDEN, D_MODEL), dtype=jnp.float32) * s
        b2 = jax.random.normal(ks[5], (N_ROUTING, D_MODEL), dtype=jnp.float32) * s
        sw1 = jax.random.normal(ks[6], (D_MODEL, HIDDEN), dtype=jnp.float32) * s
        sb1 = jax.random.normal(ks[7], (HIDDEN,), dtype=jnp.float32) * s
        sw2 = jax.random.normal(ks[8], (HIDDEN, D_MODEL), dtype=jnp.float32) * s
        sb2 = jax.random.normal(ks[9], (D_MODEL,), dtype=jnp.float32) * s
        return {'x': x, 'gate_w': gate_w, 'w1': w1, 'b1': b1, 'w2': w2, 'b2': b2, 'sw1': sw1, 'sb1': sb1, 'sw2': sw2, 'sb2': sb2}
    _L0_ffn_all = _L0_ffn_setup()
    _L0_ffn_in = {k: v for k, v in _L0_ffn_all.items() if k in ('gate_w', 'w1', 'b1', 'w2', 'b2', 'sw1', 'sb1', 'sw2', 'sb2')}
    del _L0_ffn_all
    return {'x': x, 'ctx_1024': ctx_1024, 'mask_Bx1xSxS2_ik1': mask_Bx1xSxS2_ik1, 'L0_xattn_WQ': _L0_xattn_in['WQ'], 'L0_xattn_bQ': _L0_xattn_in['bQ'], 'L0_xattn_WK': _L0_xattn_in['WK'], 'L0_xattn_bK': _L0_xattn_in['bK'], 'L0_xattn_WV': _L0_xattn_in['WV'], 'L0_xattn_bV': _L0_xattn_in['bV'], 'L0_xattn_WO': _L0_xattn_in['WO'], 'L0_xattn_bO': _L0_xattn_in['bO'], 'L0_ffn_gate_w': _L0_ffn_in['gate_w'], 'L0_ffn_w1': _L0_ffn_in['w1'], 'L0_ffn_b1': _L0_ffn_in['b1'], 'L0_ffn_w2': _L0_ffn_in['w2'], 'L0_ffn_b2': _L0_ffn_in['b2'], 'L0_ffn_sw1': _L0_ffn_in['sw1'], 'L0_ffn_sb1': _L0_ffn_in['sb1'], 'L0_ffn_sw2': _L0_ffn_in['sw2'], 'L0_ffn_sb2': _L0_ffn_in['sb2']}

def reference(x, ctx_1024, mask_Bx1xSxS2_ik1, L0_xattn_WQ, L0_xattn_bQ, L0_xattn_WK, L0_xattn_bK, L0_xattn_WV, L0_xattn_bV, L0_xattn_WO, L0_xattn_bO, L0_ffn_gate_w, L0_ffn_w1, L0_ffn_b1, L0_ffn_w2, L0_ffn_b2, L0_ffn_sw1, L0_ffn_sb1, L0_ffn_sw2, L0_ffn_sb2):
    import jax
    import jax.numpy as jnp

    def _L0_xattn_ref(query, key, value, mask, WQ, bQ, WK, bK, WV, bV, WO, bO):
        import jax, jax.numpy as jnp
        import numpy as np
        B, L, C, H = (2, 512, 256, 16)
        D = C // H
        b = query.shape[0]
        Q = query @ WQ + bQ
        K = key @ WK + bK
        V = value @ WV + bV

        def split_heads(x):
            return x.reshape(b, -1, H, D).transpose(0, 2, 1, 3)
        Qh, Kh, Vh = (split_heads(Q), split_heads(K), split_heads(V))
        scores = jnp.einsum('bhqd,bhkd->bhqk', Qh, Kh) / jnp.sqrt(jnp.float32(D))
        scores = jnp.where(mask == 0, jnp.float32(-1000000000.0), scores)
        attn = jax.nn.softmax(scores, axis=-1)
        Z = jnp.einsum('bhqk,bhkd->bhqd', attn, Vh)
        Z = Z.transpose(0, 2, 1, 3).reshape(b, Q.shape[1], C)
        return Z @ WO + bO

    def _L0_ffn_ref(x, gate_w, w1, b1, w2, b2, sw1, sb1, sw2, sb2):
        import jax, jax.numpy as jnp
        import numpy as np
        D_MODEL = 256
        HIDDEN = 1024
        N_ROUTING = 2
        B, S, D = x.shape
        xf = x.reshape(-1, D)
        gate_scores = xf @ gate_w.T
        gate_probs = jax.nn.softmax(gate_scores, axis=-1)
        top1 = jnp.argmax(gate_probs, axis=-1)
        one_hot = jax.nn.one_hot(top1, N_ROUTING, dtype=xf.dtype)
        masked = xf[None, :, :] * one_hot.T[:, :, None]
        h = jax.nn.relu(jnp.einsum('end,edh->enh', masked, w1) + b1[:, None, :])
        expert_out = jnp.einsum('enh,ehd->end', h, w2) + b2[:, None, :]
        routing_output = expert_out.sum(axis=0)
        shared = jax.nn.relu(xf @ sw1 + sb1) @ sw2 + sb2
        return (routing_output + shared).reshape(B, S, D)
    x = x + _L0_xattn_ref(_layernorm(x, axis=-1), ctx_1024, ctx_1024, mask_Bx1xSxS2_ik1, L0_xattn_WQ, L0_xattn_bQ, L0_xattn_WK, L0_xattn_bK, L0_xattn_WV, L0_xattn_bV, L0_xattn_WO, L0_xattn_bO)
    x = x + _L0_ffn_ref(_layernorm(x, axis=-1), L0_ffn_gate_w, L0_ffn_w1, L0_ffn_b1, L0_ffn_w2, L0_ffn_b2, L0_ffn_sw1, L0_ffn_sb1, L0_ffn_sw2, L0_ffn_sb2)
    return x

_drawn_inputs = setup_inputs


def setup_inputs(seed=0):
    import zlib

    import numpy as np

    out = dict(_drawn_inputs(seed))
    spreads = {'L0_xattn_bQ': (0.0, 0.304),
     'L0_xattn_bK': (0.0, 0.8),
     'L0_xattn_bV': (0.0, 0.1),
     'L0_xattn_bO': (0.0, 0.1)}
    factors = {'L0_ffn_b1': 5.939, 'L0_ffn_sb1': 7.748, 'L0_ffn_sb2': 3.216}
    for name, (base, spread) in spreads.items():
        noise = np.random.default_rng([zlib.crc32(name.encode()), seed]).standard_normal(out[name].shape)
        drawn = base * np.exp(spread * noise) if base else spread * noise
        out[name] = jnp.asarray(drawn.astype(out[name].dtype))
    for name, factor in factors.items():
        out[name] = (out[name] * factor).astype(out[name].dtype)
    return out
```

```python
import concourse.bass as bass
from concourse import mybir
from contextlib import ExitStack

F32 = mybir.dt.float32
F32R = mybir.dt.float32r
BF16 = mybir.dt.bfloat16
I32 = mybir.dt.int32
ALU = mybir.AluOpType
ACT = mybir.ActivationFunctionType
AX = mybir.AxisListType

P = 128


def attention_and_routed_ffn(nc, x, ctx, mask, WQ, bQ, WK, bK, WV, bV, WO, bO,
                             gate_w, w1, b1, w2, b2, sw1, sb1, sw2, sb2, out):
    B, S, C = x.shape
    KEYS = ctx.shape[1]
    H, D = 16, 16
    E, HID = w1.shape[0], w1.shape[3]
    KC = C // P
    TB = S // P
    NT = B * TB
    HC = HID // P
    N = B * S
    SLOTS = N + S
    ROUTED = SLOTS // S
    ROW = C + 1
    PAIRS = H // 2
    ZW = 2 * (D + 1)
    NOBODY = 1 << 20
    MASKED = -1e9
    EPS = 1e-5
    NEWTON = 3
    RSTEPS = 2 + 3 * NEWTON

    xf = x.rearrange("b (p t) c -> p b (t c)", t=TB)
    outf = out.rearrange("b s c -> (b s) c")
    maskf = mask.rearrange("b a (p t) k -> p (b a) (t k)", t=TB)
    sorted_rows = nc.dram_tensor("sorted_rows", (SLOTS, ROW), F32).ap()
    resid = nc.dram_tensor("resid", (N, C), F32).ap()
    resid_v = resid.rearrange("(b p t) c -> p b (t c)", p=P, t=TB)
    sorted_v = sorted_rows.rearrange("(f p t) c -> p f (t c)", p=P, t=TB)

    es = ExitStack()
    with es:
        def sb(name, shape, dt=F32):
            return es.enter_context(nc.sbuf_tensor(name, shape, dt))

        def sem(name):
            return es.enter_context(nc.semaphore(name))

        X = sb("X", [P, NT, C])
        cap = sb("cap", [P, NT, KEYS])
        wq = sb("wq", [P, KC, C])
        wo = sb("wo", [P, KC, C])
        kT = sb("kT", [P, KC, B * KEYS])
        kblk = sb("kblk", [P, KC, 4, KEYS])
        vblk = sb("vblk", [P, B, PAIRS * ZW])
        vcur = sb("vcur", [P, PAIRS * ZW])
        xh = sb("xh", [P, TB, C])
        xT = sb("xT", [P, KC, S])
        qT = sb("qT", [P, KC, S])
        SC = sb("SC", [P, 2, H * KEYS])
        PT = sb("PT", [P, PAIRS, P])
        Zn = sb("Zn", [P, TB, C])
        ZT = xT
        row = sb("row", [P, TB, ROW])
        stage1 = sb("stage1", [P, KC, HID])
        stage2 = sb("stage2", [P, HC, C])
        a1h = sb("a1h", [P, KC, HID], F32R)
        a1l = sb("a1l", [P, KC, HID], F32R)
        a2h = sb("a2h", [P, HC, C], F32R)
        a2l = sb("a2l", [P, HC, C], F32R)
        x2h = sb("x2h", [P, KC, S], F32R)
        x2l = sb("x2l", [P, KC, S], F32R)
        hf = sb("hf", [P, 2, S])
        hh = sb("hh", [P, HC, S], F32R)
        hl = sb("hl", [P, HC, S], F32R)
        shared_region = sb("shared_region", [P, 2 * 4 * P * KC + TB * C])
        ctx_nat = shared_region[:, 0:TB * C].rearrange("p (j c) -> p j c", c=C)
        ctxT2 = shared_region[:, TB * C:TB * C + KC * B * 2 * KEYS].rearrange(
            "p (k b d n) -> p k b d n", k=KC, b=B, d=2)
        wk = stage1[:, 0, 0:KC * C].rearrange("p (k c) -> p k c", k=KC)
        wv = stage1[:, 1, 0:KC * C].rearrange("p (k c) -> p k c", k=KC)
        rg = shared_region[:, 0:TB * C].rearrange("p (j c) -> p j c", c=C)
        xg = shared_region[:, TB * C:TB * C + TB * ROW].rearrange("p (j c) -> p j c", c=ROW)
        bo_b = sb("bo_b", [P, C])
        bv_b = sb("bv_b", [P, C])
        gw_b = sb("gw_b", [P, E, C])
        crow = sb("crow", [P, E, C])
        crow_cur = sb("crow_cur", [P, C])
        bq_c = sb("bq_c", [P, KC])
        bk_c = sb("bk_c", [P, KC])
        b1_c = sb("b1_c", [P, E, HC])
        b1_cur = sb("b1_cur", [P, HC])
        rb1 = sb("rb1", [P, E, HC])
        ident = sb("ident", [P, P])
        tri = sb("tri", [P, P], BF16)
        ones = sb("ones", [P, P], BF16)
        dmask = sb("dmask", [P, 4])
        tok_i = sb("tok_i", [P, NT], I32)
        ord_i = sb("ord_i", [P, NT], I32)
        tok_f = sb("tok_f", [P, NT])
        tok_r = sb("tok_r", [P, NT])
        tile_i = sb("tile_i", [P, ROUTED], I32)
        tile_f = sb("tile_f", [P, ROUTED])
        exp_f = sb("exp_f", [P, ROUTED])
        exp_i = sb("exp_i", [P, ROUTED], I32)
        n0 = sb("n0", [P, 1])
        fill = sb("fill", [P, ROW])
        stA, stB = sb("stA", [P, TB, 6]), sb("stB", [P, TB, 6])
        mvA, mvB = sb("mvA", [P, TB, 2]), sb("mvB", [P, TB, 2])
        rsA, rsB = sb("rsA", [P, TB]), sb("rsB", [P, TB])
        rv, rt = sb("rv", [P, TB]), sb("rt", [P, TB])
        mx = sb("mx", [P, 2, H])
        rec = sb("rec", [P, 2, H])
        gsc = sb("gsc", [P, TB, E])
        sel = sb("sel", [P, TB + 1], BF16)
        R = sb("R", [P, TB + 1], BF16)

        rsum = sb("rsum", [P, 1])
        slotA, slotB = sb("slotA", [P, TB]), sb("slotB", [P, TB])
        slot_i = sb("slot_i", [P, TB], I32)
        ids = sb("ids", [P, TB], I32)

        ps = es.enter_context(nc.psum_tensor("ps", [P, 8, 512], F32))
        U = [ps[:, 0, :], ps[:, 1, :]]
        Sb = ps[:, 2:4, :]
        A = [ps[:, 4, :], ps[:, 5, :]]
        Zb = [ps[:, 6, :], ps[:, 7, :]]

        names = """d_x d_ctx d_wk d_wv d_wq d_wo d_mask d_vec d_w2e d_stage1 d_stage2 d_b1 d_fill d_res
            d_scat d_xg d_rg d_crow d_out
            p_ident p_dmask p_tabs p_cap0 p_cap p_fill p_vz p_kb p_xb p_sub p_rowid p_ids p_rgc p_sel0
            v_ctxT v_kT v_vb v_tok v_tokr v_cvec v_rb1 v_crow0 v_crow v_st1 v_mv1 v_rs1 v_xh v_min v_max v_x2l v_hh v_hl
            v_rec v_zn v_y v_x1 v_st2 v_mv2 v_rs2 v_row v_gate v_sel v_sa v_sb v_slot v_rsum v_R v_n0 v_exp
            v_expi v_w1l v_w2l v_rbx
            a_rbc a_xT a_qT a_exp a_PT a_ZT a_x2h a_hf a_w1h a_w2h
            t_ctx t_k t_v t_const t_T1 t_q t_s t_PT t_z t_ZT t_wo t_rank t_T2 t_up t_down""".split()
        s = {n: sem(n) for n in names}

        def halves(bank):
            return bank.rearrange("p (j c) -> p j c", c=C)

        rbc = [hf[:, :, :].rearrange("p a n -> p (a n)").rearrange("p (c m) -> p c m", m=P),
               row[:, :, :].rearrange("p a n -> p (a n)")[:, 0:HC * P].rearrange("p (c m) -> p c m", m=P)]
        w2e = X[:, NT // 2:NT, :].rearrange("p (e j) c -> p e j c", e=E)

        block = es.enter_context(nc.Block())

        @block.sync
        def _(sp):
            sp.dma_start(ctx_nat, ctx.rearrange("b k c -> (b k) c").rearrange("(j p) c -> p j c", p=P)).then_inc(s["d_ctx"], 16)
            sp.dma_start(X[:, 0:TB, :].rearrange("p t c -> p (t c)"), xf[:, 0, :]).then_inc(s["d_x"], 16)
            sp.dma_start(wk, WK).then_inc(s["d_wk"], 16)
            sp.dma_start(wv, WV).then_inc(s["d_wv"], 16)
            sp.dma_start(wq[:], WQ).then_inc(s["d_wq"], 16)
            sp.dma_start(cap[:, :, :].bitcast(I32).rearrange("p (b t) k -> p b (t k)", t=TB), maskf).then_inc(s["d_mask"], 16)
            sp.dma_start(w2e, w2.rearrange("e p j c -> p e j c")).then_inc(s["d_w2e"], 16)
            sp.dma_start(wo[:], WO).then_inc(s["d_wo"], 16)
            for b in range(1, B // 2):
                sp.wait_ge(s["d_x"], 16 * b)
                sp.dma_start(X[:, TB * b:TB * b + TB, :].rearrange("p t c -> p (t c)"), xf[:, b, :]).then_inc(s["d_x"], 16)
            sp.wait_ge(s["t_v"], 4)
            sp.dma_start(stage1[:], sw1).then_inc(s["d_stage1"], 16)
            sp.dma_start(stage2[:], sw2).then_inc(s["d_stage2"], 16)
            sp.wait_ge(s["p_fill"], 2)
            sp.dma_start(sorted_rows.rearrange("(p r) c -> p r c", p=P),
                         fill[:, :].unsqueeze(1).broadcast_to([P, SLOTS // P, ROW])).then_inc(s["d_fill"], 16)
            sp.wait_ge(s["t_const"], 2)
            for b in range(B // 2, B):
                sp.wait_ge(s["d_x"], 16 * b)
                sp.dma_start(X[:, TB * b:TB * b + TB, :].rearrange("p t c -> p (t c)"), xf[:, b, :]).then_inc(s["d_x"], 16)
            def resid_out(b):
                sp.wait_ge(s["v_y"], b * 4 + 4)
                sp.dma_start(resid_v[:, bass.ds(b, 1), :].rearrange("p b n -> p (b n)"),
                             X[:, bass.ds(b * TB, TB), :].rearrange("p t c -> p (t c)")).then_inc(s["d_res"], 16)

            def routed_in(t):
                e = sp.value_load(exp_i[0:1, bass.ds(t, 1)], min_val=0, max_val=E - 1)
                sp.wait_ge(s["v_w1l"], t + 1)
                sp.dma_start(stage1[:], w1[bass.ds(e, 1), :, :, :].rearrange("e p k n -> (e p) k n")).then_inc(s["d_stage1"], 16)
                sp.wait_ge(s["v_w2l"], t + 1)
                sp.dma_start(stage2[:], w2[bass.ds(e, 1), :, :, :].rearrange("e p j c -> (e p) j c")).then_inc(s["d_stage2"], 16)
                sp.wait_ge(s["p_ids"], t + 1)
                sp.wait_ge(s["t_T2"], t * 2 + 2 * B)
                sp.dma_start(xg.rearrange("p j c -> p (j c)"), sorted_v[:, bass.ds(t, 1), :].rearrange("p f n -> p (f n)")).then_inc(s["d_xg"], 16)
                sp.wait_ge(s["a_hf"], t * 8 + 8 * B)
                sp.dma_start(b1_cur[:], b1_c[:, bass.ds(e, 1), :].rearrange("p e j -> p (e j)")).then_inc(s["d_b1"], 16)
                sp.wait_ge(s["p_rgc"], t + 1)
                sp.dma_start(crow_cur[:], crow[:, bass.ds(e, 1), :].rearrange("p e c -> p (e c)")).then_inc(s["d_crow"], 16)

            with sp.Fori(0, B - 1) as b:
                resid_out(b)
            sp.wait_ge(s["v_expi"], 1)
            sp.wait_ge(s["d_scat"], 64 * B)
            routed_in(0)
            resid_out(B - 1)
            with sp.Fori(1, ROUTED) as t:
                routed_in(t)
            sp.wait_ge(s["d_res"], 16 * B)
            sp.wait_ge(s["d_out"], 64 * ROUTED)

        @block.gpsimd
        def _(pool):
            g = nc.gpsimd
            g.memset(ones[:], 1.0).then_inc(s["p_ident"], 1)
            g.memset(dmask[:], 1.0).then_inc(s["p_ident"], 1)
            pool.wait_ge(s["p_ident"], 2)
            g.affine_select(out=ident[:], in_=ones[:], compare_op=ALU.is_equal, fill=0.0, base=0,
                            pattern=[[-1, P]], channel_multiplier=1).then_inc(s["p_ident"], 1)
            g.affine_select(out=tri[:], in_=ones[:], compare_op=ALU.is_gt, fill=0.0, base=0,
                            pattern=[[1, P]], channel_multiplier=-1).then_inc(s["p_ident"], 1)
            pool.wait_ge(s["p_ident"], 4)
            for r in range(2):
                g.affine_select(out=dmask[64 * r:64 * r + 64, :], in_=dmask[64 * r:64 * r + 64, :], compare_op=ALU.is_ge,
                                fill=0.0, base=0, pattern=[[-D, 4]], channel_multiplier=1).then_inc(s["p_dmask"], 1)
            pool.wait_ge(s["p_dmask"], 2)
            for r in range(2):
                g.affine_select(out=dmask[64 * r:64 * r + 64, :], in_=dmask[64 * r:64 * r + 64, :], compare_op=ALU.is_ge,
                                fill=0.0, base=D - 1, pattern=[[D, 4]], channel_multiplier=-1).then_inc(s["p_dmask"], 1)
            pool.wait_ge(s["p_dmask"], 4)
            g.memset(vblk[:], 0.0).then_inc(s["p_vz"], 1)
            pool.wait_ge(s["p_vz"], 1)
            vv = vblk[:, :, :].rearrange("p b (r w) -> p b r w", w=ZW)
            g.memset(vv[0:KEYS, :, :, D:D + 1], 1.0).then_inc(s["p_vz"], 1)
            g.memset(vv[KEYS:P, :, :, ZW - 1:ZW], 1.0).then_inc(s["p_vz"], 1)
            pool.wait_ge(s["p_vz"], 3)
            pool.wait_ge(s["d_mask"], 16)
            g.tensor_scalar(cap[:], cap[:, :, :].bitcast(I32), 0.0, -2e30, ALU.is_equal, ALU.mult).then_inc(s["p_cap0"], 1)
            pool.wait_ge(s["p_cap0"], 1)
            g.tensor_scalar(cap[:], cap[:], 1e30, MASKED, ALU.add, ALU.max).then_inc(s["p_cap"], 1)
            g.iota(tok_i[:], pattern=[[S, B], [1, TB]], base=0, channel_multiplier=TB).then_inc(s["p_tabs"], 1)
            g.iota(ord_i[:], pattern=[[P, NT]], base=0, channel_multiplier=1).then_inc(s["p_tabs"], 1)
            g.iota(tile_i[:], pattern=[[S, ROUTED]], base=0, channel_multiplier=0).then_inc(s["p_tabs"], 1)
            g.memset(sel[:], 0.0).then_inc(s["p_sel0"], 1)
            g.memset(R[:], 0.0).then_inc(s["p_sel0"], 1)
            g.memset(fill[:, 0:C], 0.0).then_inc(s["p_fill"], 1)
            g.memset(fill[:, C:ROW].bitcast(I32), NOBODY).then_inc(s["p_fill"], 1)

            def keys_of(b):
                pool.wait_ge(s["v_kT"], 2)
                pool.wait_ge(s["p_dmask"], 4)
                pool.wait_ge(s["v_vb"], 16)
                pool.wait_ge(s["p_vz"], 3)
                pool.wait_ge(s["d_x"], b * 16 + 16)
                pool.wait_ge(s["d_vec"], 7 * 16)
                pool.wait_ge(s["v_xh"], b + 1)
                g.tensor_tensor(X[:, bass.ds(b * TB, TB), :], X[:, bass.ds(b * TB, TB), :],
                                bo_b[:, :].unsqueeze(1).broadcast_to([P, TB, C]), ALU.add).then_inc(s["p_xb"], 1)

            def keys_build(b, first):
                if not first:
                    pool.wait_ge(s["t_s"], b * 4)
                    pool.wait_ge(s["t_z"], b * 4)
                g.tensor_tensor(kblk[:], kT[:, :, bass.ds(b * KEYS, KEYS)].unsqueeze(2).broadcast_to([P, KC, 4, KEYS]),
                                dmask[:, :].unsqueeze(1).unsqueeze(3).broadcast_to([P, KC, 4, KEYS]),
                                ALU.mult).then_inc(s["p_kb"], 1)
                g.tensor_copy(vcur[:], vblk[:, bass.ds(b, 1), :].rearrange("p b w -> p (b w)")).then_inc(s["p_kb"], 1)

            def subtract_max(b, i):
                pool.wait_ge(s["v_max"], b * 4 + i + 1)
                sc = SC[:, i % 2, :].rearrange("p (h k) -> p h k", k=KEYS)
                g.tensor_tensor(sc, sc, mx[:, i % 2, :].unsqueeze(2).broadcast_to([P, H, KEYS]),
                                ALU.subtract).then_inc(s["p_sub"], 1)

            def scatter(f):
                pool.wait_ge(s["v_row"], f * 4 + 4)
                g.tensor_copy(row[:, :, C].bitcast(I32), tok_i[:, bass.ds(f * TB, TB)]).then_inc(s["p_rowid"], 1)
                pool.wait_ge(s["d_fill"], 16)
                pool.wait_ge(s["p_rowid"], f + 1)
                pool.wait_ge(s["v_slot"], f + 1)
                for j in range(TB):
                    g.indirect_dma_start(out=sorted_rows, out_offset=bass.IndirectOffsetOnAxis(ap=slot_i[:, j:j + 1], axis=0),
                                         in_=row[:, j, :], in_offset=None).then_inc(s["d_scat"], 16)
                pool.wait_ge(s["d_scat"], f * 64 + 64)

            def attention(b, first):
                keys_build(b, first)
                keys_of(b)
                subtract_max(b, 0)
                subtract_max(b, 1)
                if not first:
                    scatter(b - 1)
                subtract_max(b, 2)
                subtract_max(b, 3)

            pool.wait_ge(s["v_kT"], 2)
            pool.wait_ge(s["p_dmask"], 4)
            pool.wait_ge(s["v_vb"], 16)
            pool.wait_ge(s["p_vz"], 3)
            attention(0, True)
            with pool.Fori(1, B) as b:
                attention(b, False)
            scatter(B - 1)
            pool.wait_ge(s["t_ctx"], 2)
            pool.wait_ge(s["t_v"], 4)
            g.memset(rg[:, 0:2, :], 0.0).then_inc(s["p_ids"], 1)
            g.memset(rg[:, 2:4, :], 0.0).then_inc(s["p_rgc"], 1)
            pool.wait_ge(s["p_ids"], 1)
            with pool.Fori(0, ROUTED) as t:
                pool.compute_val(t * 16 + 16)
                pool.wait_ge(s["d_xg"], 16)
                pool.wait_ge(s["d_xg"], t * 16 + 16)
                g.tensor_copy(ids[:], xg[:, :, C].bitcast(I32)).then_inc(s["p_ids"], 1)
                pool.compute_val(t + 2)
                pool.wait_ge(s["d_res"], 16 * B)
                pool.wait_ge(s["p_ids"], t + 2)
                for j in range(TB):
                    g.indirect_dma_start(out=rg[:, j, :], out_offset=None, in_=resid,
                                         in_offset=bass.IndirectOffsetOnAxis(ap=ids[:, j:j + 1], axis=0),
                                         bounds_check=N - 1, oob_is_err=False).then_inc(s["d_rg"], 16)
                pool.wait_ge(s["d_rg"], t * 64 + 64)
                pool.wait_ge(s["d_crow"], t * 16 + 16)
                g.tensor_tensor(rg, rg, crow_cur[:, :].unsqueeze(1).broadcast_to([P, TB, C]), ALU.add).then_inc(s["p_rgc"], 1)
                for j in range(TB):
                    pool.compute_val(t * 4 + (4 * B + j + 1))
                    pool.wait_ge(s["v_y"], 4 * B)
                    pool.wait_ge(s["v_y"], t * 4 + (4 * B + j + 1))
                    g.indirect_dma_start(out=outf, out_offset=bass.IndirectOffsetOnAxis(ap=ids[:, j:j + 1], axis=0),
                                         in_=rg[:, j, :], in_offset=None,
                                         bounds_check=N - 1, oob_is_err=False).then_inc(s["d_out"], 16)
                pool.wait_ge(s["d_out"], t * 64 + 64)

        @block.scalar
        def _(act):
            a = nc.scalar
            act.dma_start(bk_c[:], bK).then_inc(s["d_vec"], 16)
            act.dma_start(bv_b[:], bV.partition_broadcast(P)).then_inc(s["d_vec"], 16)
            act.dma_start(bq_c[:], bQ).then_inc(s["d_vec"], 16)
            act.dma_start(b1_c[:], b1).then_inc(s["d_vec"], 16)
            act.dma_start(bo_b[:], bO.partition_broadcast(P)).then_inc(s["d_vec"], 16)
            act.dma_start(gw_b[:], gate_w.partition_broadcast(P)).then_inc(s["d_vec"], 16)
            act.dma_start(crow[:], b2.partition_broadcast(P)).then_inc(s["d_vec"], 16)
            act.dma_start(crow_cur[:], sb2.partition_broadcast(P)).then_inc(s["d_vec"], 16)
            act.dma_start(b1_cur[:], sb1).then_inc(s["d_b1"], 16)

            def queries_T(b):
                for k in range(KC):
                    act.wait_ge(s["t_T1"], b * 2 + k + 1)
                    act.wait_ge(s["t_wo"], b * 2)
                    a.activation(xT[:, k, :], Sb[:, k, :], ACT.Copy).then_inc(s["a_xT"], 1)

            def project_q(b):
                for m in range(KC):
                    act.wait_ge(s["t_q"], b * 2 + m + 1)
                    a.activation(qT[:, m, :], A[m], ACT.Identity, bias=bq_c[:, m:m + 1]).then_inc(s["a_qT"], 1)

            def expo(b, i):
                act.wait_ge(s["p_sub"], b * 4 + i + 1)
                a.activation(SC[:, i % 2, :], SC[:, i % 2, :], ACT.Exp).then_inc(s["a_exp"], 1)

            def probs_T(b, i):
                for hlf in range(2):
                    act.wait_ge(s["t_PT"], b * 8 + 2 * i + hlf + 1)
                    if i > 0 and hlf == 0:
                        act.wait_ge(s["t_z"], b * 4 + i)
                    a.activation(PT[:, 4 * hlf:4 * hlf + 4, :].rearrange("p a n -> p (a n)"), A[hlf], ACT.Copy).then_inc(s["a_PT"], 1)

            def z_T(b):
                for k in range(KC):
                    act.wait_ge(s["t_ZT"], b * 2 + k + 1)
                    a.activation(ZT[:, k, :], A[k], ACT.Copy).then_inc(s["a_ZT"], 1)

            def ffn_in_high(f):
                for k in range(KC):
                    act.wait_ge(s["t_T2"], f * 2 + k + 1)
                    a.activation(x2h[:, k, :], A[k], ACT.Copy).then_inc(s["a_x2h"], 1)

            def hidden(f, c):
                act.wait_ge(s["t_up"], f * 8 + c + 1)
                if c >= 2:
                    act.wait_ge(s["v_hl"], f * 8 + c - 1)
                a.activation(hf[:, c % 2, :], U[c % 2], ACT.Relu, bias=b1_cur[:, c:c + 1]).then_inc(s["a_hf"], 1)

            def attention(b, first, last):
                project_q(b)
                if not first:
                    f = b - 1
                    ffn_in_high(f)
                    hidden(f, 0)
                expo(b, 0)
                if not first:
                    hidden(f, 1)
                    hidden(f, 2)
                probs_T(b, 0)
                expo(b, 1)
                if not first:
                    hidden(f, 3)
                    hidden(f, 4)
                expo(b, 2)
                probs_T(b, 1)
                if not first:
                    hidden(f, 5)
                probs_T(b, 2)
                expo(b, 3)
                if not first:
                    hidden(f, 6)
                    hidden(f, 7)
                probs_T(b, 3)
                z_T(b)
                if not last:
                    queries_T(b + 1)

            act.wait_ge(s["d_vec"], 8 * 16)
            act.wait_ge(s["v_rb1"], 1)
            for e in range(E):
                a.activation(rbc[e], rb1[:, e, :].unsqueeze(2).broadcast_to([P, HC, P]), ACT.Copy).then_inc(s["a_rbc"], 1)
            for k in range(KC):
                act.wait_ge(s["t_T1"], k + 1)
                a.activation(xT[:, k, :], Sb[:, k, :], ACT.Copy).then_inc(s["a_xT"], 1)
            attention(0, True, False)
            act.wait_ge(s["d_stage1"], 16)
            a.activation(a1h[:], stage1[:], ACT.Copy).then_inc(s["a_w1h"], 1)
            act.wait_ge(s["d_stage2"], 16)
            a.activation(a2h[:], stage2[:], ACT.Copy).then_inc(s["a_w2h"], 1)
            act.wait_ge(s["d_b1"], 16)
            with act.Fori(1, B - 1) as b:
                attention(b, False, False)
            attention(B - 1, False, True)
            ffn_in_high(B - 1)
            for c in range(HC):
                hidden(B - 1, c)
            act.wait_ge(s["d_stage1"], 32)
            a.activation(a1h[:], stage1[:], ACT.Copy).then_inc(s["a_w1h"], 1)

            def routed(t, last):
                f = t + B
                ffn_in_high(f)
                act.wait_ge(s["d_b1"], t * 16 + 32)
                for c in range(HC):
                    hidden(f, c)
                    if c == 2:
                        act.wait_ge(s["d_stage2"], t * 16 + 32)
                        act.wait_ge(s["t_down"], f * 4)
                        a.activation(a2h[:], stage2[:], ACT.Copy).then_inc(s["a_w2h"], 1)
                if not last:
                    act.wait_ge(s["d_stage1"], t * 16 + 48)
                    a.activation(a1h[:], stage1[:], ACT.Copy).then_inc(s["a_w1h"], 1)

            with act.Fori(0, ROUTED - 1) as t:
                routed(t, False)
            routed(ROUTED - 1, True)

        @block.vector
        def _(dve):
            v = nc.vector

            def inverse_root(b, mv, rs, done):
                v.tensor_scalar(rv[:], mv[:, :, 1], EPS, None, ALU.add).then_inc(done, 1)
                dve.wait_ge(done, b * RSTEPS + 1)
                v.tensor_scalar(rs[:, :].bitcast(I32), rv[:, :].bitcast(I32), -0.5, float(0x5F3759DF),
                                ALU.mult, ALU.add).then_inc(done, 1)
                dve.wait_ge(done, b * RSTEPS + 2)
                for k in range(NEWTON):
                    v.tensor_tensor(rt[:], rs[:], rs[:], ALU.mult).then_inc(done, 1)
                    dve.wait_ge(done, b * RSTEPS + 3 * k + 3)
                    v.scalar_tensor_tensor(out=rt[:], in0=rt[:], scalar=-0.5, in1=rv[:], op0=ALU.mult, op1=ALU.mult).then_inc(done, 1)
                    dve.wait_ge(done, b * RSTEPS + 3 * k + 4)
                    v.scalar_tensor_tensor(out=rs[:], in0=rt[:], scalar=1.5, in1=rs[:], op0=ALU.add, op1=ALU.mult).then_inc(done, 1)
                    dve.wait_ge(done, b * RSTEPS + 3 * k + 5)

            def norm1(b):
                dve.wait_ge(s["d_x"], 16)
                dve.wait_ge(s["d_x"], b * 16 + 16)
                for i in range(TB):
                    last = v.bn_stats(stA[:, i, :], X[:, bass.ds(b * TB + i, 1), :].rearrange("p a c -> p (a c)"))
                last.then_inc(s["v_st1"], 1)
                dve.compute_val(b + 1)
                dve.wait_ge(s["v_st1"], 1)
                dve.wait_ge(s["v_st1"], b + 1)
                for i in range(TB):
                    last = v.bn_aggr(mvA[:, i, :], stA[:, i, :])
                last.then_inc(s["v_mv1"], 1)
                dve.wait_ge(s["v_mv1"], b + 1)
                inverse_root(b, mvA, rsA, s["v_rs1"])
                if not isinstance(b, int) or b > 0:
                    dve.wait_ge(s["t_T1"], b * 2)
                for i in range(TB):
                    last = v.tensor_scalar(xh[:, i, :], X[:, bass.ds(b * TB + i, 1), :].rearrange("p a c -> p (a c)"),
                                           mvA[:, i, 0:1], rsA[:, i:i + 1], ALU.subtract, ALU.mult)
                last.then_inc(s["v_xh"], 1)

            def masked_max(b, i, first):
                dve.wait_ge(s["t_s"], b * 4 + i + 1)
                if i >= 2:
                    dve.wait_ge(s["t_PT"], b * 8 + 2 * i - 2)
                elif not first:
                    dve.wait_ge(s["t_PT"], b * 8 - 4 + 2 * i)
                sc = SC[:, i % 2, :].rearrange("p (h k) -> p h k", k=KEYS)
                v.tensor_tensor(sc, Sb.rearrange("p s (h k) -> p (s h) k", k=KEYS),
                                cap[:, bass.ds(b * TB + i, 1), :].broadcast_to([P, H, KEYS]), ALU.min).then_inc(s["v_min"], 1)
                dve.wait_ge(s["v_min"], b * 4 + i + 1)
                v.tensor_reduce(mx[:, i % 2, :], sc, AX.X, ALU.max).then_inc(s["v_max"], 1)

            def normalise(b, i):
                dve.wait_ge(s["t_z"], b * 4 + i + 1)
                z = Zb[i % 2][:, 0:H * (D + 1)].rearrange("p (h w) -> p h w", w=D + 1)
                v.reciprocal(rec[:, i % 2, :], z[:, :, D]).then_inc(s["v_rec"], 1)
                dve.wait_ge(s["v_rec"], b * 4 + i + 1)
                v.tensor_tensor(Zn[:, i, :].rearrange("p (h d) -> p h d", d=D), z[:, :, 0:D],
                                rec[:, i % 2, :].unsqueeze(2).broadcast_to([P, H, D]), ALU.mult).then_inc(s["v_zn"], 1)

            def attended(b):
                dve.wait_ge(s["p_xb"], b + 1)
                for h in range(2):
                    dve.wait_ge(s["t_wo"], b * 2 + h + 1)
                    xs = X[:, bass.ds(b * TB + 2 * h, 2), :]
                    v.tensor_tensor(xs, halves(A[h]), xs, ALU.add).then_inc(s["v_x1"], 1)

            def norm2(b, first):
                dve.wait_ge(s["v_x1"], 2)
                dve.wait_ge(s["v_x1"], b * 2 + 2)
                for i in range(TB):
                    last = v.bn_stats(stB[:, i, :], X[:, bass.ds(b * TB + i, 1), :].rearrange("p a c -> p (a c)"))
                last.then_inc(s["v_st2"], 1)
                dve.compute_val(b + 1)
                dve.wait_ge(s["v_st2"], 1)
                dve.wait_ge(s["v_st2"], b + 1)
                for i in range(TB):
                    last = v.bn_aggr(mvB[:, i, :], stB[:, i, :])
                last.then_inc(s["v_mv2"], 1)
                dve.wait_ge(s["v_mv2"], b + 1)
                inverse_root(b, mvB, rsB, s["v_rs2"])
                if not first:
                    dve.wait_ge(s["d_scat"], b * 64)
                    dve.wait_ge(s["t_T2"], b * 2)
                for i in range(TB):
                    v.tensor_scalar(row[:, i, 0:C], X[:, bass.ds(b * TB + i, 1), :].rearrange("p a c -> p (a c)"),
                                    mvB[:, i, 0:1], rsB[:, i:i + 1], ALU.subtract, ALU.mult).then_inc(s["v_row"], 1)

            def gate(b, e):
                dve.wait_ge(s["v_row"], b * 4 + 4)
                for i in range(TB):
                    if e > 0:
                        dve.wait_ge(s["v_gate"], b * 8 + i + 1)
                    v.tensor_tensor_reduce(out=Zn[:, i, :], in0=row[:, i, 0:C], in1=gw_b[:, e, :], scale=1.0, scalar=0.0,
                                           op0=ALU.mult, op1=ALU.add, accum_out=gsc[:, i, e:e + 1]).then_inc(s["v_gate"], 1)

            def choose(b):
                dve.wait_ge(s["v_gate"], b * 8 + 8)
                v.tensor_tensor(sel[:, 0:TB], gsc[:, :, 1], gsc[:, :, 0], ALU.is_gt).then_inc(s["v_sel"], 1)

            def slots(f):
                dve.wait_ge(s["t_rank"], f + 1)
                r = Zb[1][:, 0:TB]
                v.scalar_tensor_tensor(out=slotA[:], in0=r, scalar=-1.0, in1=tok_f[:, bass.ds(f * TB, TB)],
                                       op0=ALU.mult, op1=ALU.add).then_inc(s["v_sa"], 1)
                v.tensor_tensor(slotB[:], sel[:, 0:TB], tok_r[:, bass.ds(f * TB, TB)], ALU.mult).then_inc(s["v_sb"], 1)
                v.tensor_reduce(rsum[:], sel[:, 0:TB], AX.X, ALU.add).then_inc(s["v_rsum"], 1)
                dve.wait_ge(s["v_sa"], f + 1)
                dve.wait_ge(s["v_sb"], f + 1)
                v.tensor_tensor(slot_i[:], slotA[:], slotB[:], ALU.add).then_inc(s["v_slot"], 1)
                dve.wait_ge(s["v_rsum"], f + 1)
                v.tensor_tensor(R[:], R[:], rsum[:, :].broadcast_to([P, TB + 1]), ALU.add).then_inc(s["v_R"], 1)

            def ffn_in_low(f):
                for k in range(KC):
                    dve.wait_ge(s["a_x2h"], f * 2 + k + 1)
                    v.tensor_tensor(x2l[:, k, :], A[k], x2h[:, k, :].bitcast(F32), ALU.subtract).then_inc(s["v_x2l"], 1)

            def hidden_split(f, c):
                dve.wait_ge(s["a_hf"], f * 8 + c + 1)
                v.tensor_copy(hh[:, c, :], hf[:, c % 2, :]).then_inc(s["v_hh"], 1)
                dve.wait_ge(s["v_hh"], f * 8 + c + 1)
                v.tensor_tensor(hl[:, c, :], hf[:, c % 2, :], hh[:, c, :].bitcast(F32), ALU.subtract).then_inc(s["v_hl"], 1)

            def shared_out(f, d):
                dve.wait_ge(s["t_down"], f * 4 + d + 1)
                xs = X[:, bass.ds(f * TB + d, 1), :].rearrange("p a c -> p (a c)")
                v.tensor_tensor(xs, U[d % 2][:, 0:C], xs, ALU.add).then_inc(s["v_y"], 1)

            def split_low(w):
                if w == 1:
                    v.tensor_tensor(a1l[:], stage1[:], a1h[:, :, :].bitcast(F32), ALU.subtract).then_inc(s["v_w1l"], 1)
                else:
                    v.tensor_tensor(a2l[:], stage2[:], a2h[:, :, :].bitcast(F32), ALU.subtract).then_inc(s["v_w2l"], 1)

            def attention(b, first, last):
                masked_max(b, 0, first)
                if not first:
                    f = b - 1
                    ffn_in_low(f)
                masked_max(b, 1, first)
                if not first:
                    gate(f, 0)
                    hidden_split(f, 0)
                    gate(f, 1)
                    hidden_split(f, 1)
                    choose(f)
                    hidden_split(f, 2)
                masked_max(b, 2, first)
                if not first:
                    slots(f)
                normalise(b, 0)
                if not first:
                    hidden_split(f, 3)
                    hidden_split(f, 4)
                masked_max(b, 3, first)
                if not first:
                    hidden_split(f, 5)
                normalise(b, 1)
                if not last:
                    norm1(b + 1)
                if not first:
                    hidden_split(f, 6)
                    hidden_split(f, 7)
                normalise(b, 2)
                normalise(b, 3)
                if not first:
                    shared_out(f, 0)
                    shared_out(f, 1)
                    shared_out(f, 2)
                attended(b)
                if not first:
                    shared_out(f, 3)
                norm2(b, first)

            for k in range(KC):
                dve.wait_ge(s["t_ctx"], k + 1)
                src = A[k].rearrange("p (b n) -> p b n", n=KEYS)
                for d in range(2):
                    last = v.tensor_copy(ctxT2[:, k, :, d, :], src)
                last.then_inc(s["v_ctxT"], 1)
            norm1(0)
            dve.wait_ge(s["d_vec"], 8 * 16)
            for m in range(KC):
                dve.wait_ge(s["t_k"], m + 1)
                v.tensor_scalar(kT[:, m, :], Zb[m], bk_c[:, m:m + 1], 0.25, ALU.add, ALU.mult).then_inc(s["v_kT"], 1)
            dve.wait_ge(s["p_vz"], 3)
            vb = vblk[:, :, :].rearrange("p b (r o w) -> p b r o w", o=2, w=D + 1)
            vbank = [U[0], U[1], Sb[:, 0, :], Sb[:, 1, :]]
            for b in range(B):
                dve.wait_ge(s["t_v"], b // 2 + 1)
                src = vbank[b // 2][:, (b % 2) * C:(b % 2) * C + C].rearrange("p (r o d) -> p r o d", o=2, d=D)
                bias = bv_b[:, :].rearrange("p (r o d) -> p r o d", o=2, d=D)
                for o in range(2):
                    q = slice(64 * o, 64 * o + 64)
                    v.tensor_tensor(vb[q, b, :, o, 0:D], src[q, :, o, :], bias[q, :, o, :], ALU.add).then_inc(s["v_vb"], 1)
            v.tensor_scalar(rb1[:], b1_c[:], 0.0, None, ALU.max).then_inc(s["v_rb1"], 1)
            dve.wait_ge(s["p_tabs"], 3)
            v.tensor_copy(tok_f[:], ord_i[:]).then_inc(s["v_tok"], 1)
            v.tensor_copy(tile_f[:], tile_i[:])
            dve.wait_ge(s["v_tok"], 1)
            v.tensor_scalar(tok_r[:], tok_f[:], -1.0, float(SLOTS - 1), ALU.mult, ALU.add).then_inc(s["v_tokr"], 1)
            v.tensor_tensor(crow_cur[:], crow_cur[:], crow[:, 0, :], ALU.add).then_inc(s["v_cvec"], 1)
            dve.wait_ge(s["v_cvec"], 1)
            v.tensor_tensor(crow_cur[:], crow_cur[:], crow[:, 1, :], ALU.add).then_inc(s["v_cvec"], 1)
            dve.wait_ge(s["v_cvec"], 2)
            dve.wait_ge(s["v_tokr"], 1)
            dve.wait_ge(s["p_cap"], 1)
            dve.wait_ge(s["p_sel0"], 2)
            attention(0, True, False)
            for e in range(E):
                dve.wait_ge(s["t_const"], e + 1)
                v.tensor_tensor(crow[:, 1 - e, :], U[e][:, 0:C], crow_cur[:], ALU.add).then_inc(s["v_crow"], 1)
            dve.wait_ge(s["a_w1h"], 1)
            split_low(1)
            dve.wait_ge(s["a_w2h"], 1)
            split_low(2)
            with dve.Fori(1, B - 1) as b:
                attention(b, False, False)
            attention(B - 1, False, True)
            ffn_in_low(B - 1)
            gate(B - 1, 0)
            gate(B - 1, 1)
            choose(B - 1)
            slots(B - 1)
            v.tensor_scalar(n0[:], Zb[1][:, TB:TB + 1], -1.0, float(N), ALU.mult, ALU.add).then_inc(s["v_n0"], 1)
            dve.wait_ge(s["v_n0"], 1)
            v.tensor_scalar(exp_f[:], tile_f[:], n0[:, 0:1], None, ALU.is_ge).then_inc(s["v_exp"], 1)
            dve.wait_ge(s["v_exp"], 1)
            v.tensor_copy(exp_i[:], exp_f[:]).then_inc(s["v_expi"], 1)
            for c in range(HC):
                hidden_split(B - 1, c)
            dve.wait_ge(s["a_w1h"], 2)
            split_low(1)
            ffn_in_low(B)
            for d in range(TB):
                shared_out(B - 1, d)

            def routed(t, last):
                f = t + B
                for c in range(HC):
                    hidden_split(f, c)
                    if c == 2:
                        dve.wait_ge(s["a_w2h"], t + 2)
                        split_low(2)
                if not last:
                    dve.wait_ge(s["a_w1h"], t + 3)
                    split_low(1)
                    ffn_in_low(f + 1)
                dve.wait_ge(s["p_rgc"], t + 2)
                for d in range(TB):
                    dve.wait_ge(s["t_down"], f * 4 + d + 1)
                    v.tensor_tensor(rg[:, d, :], U[d % 2][:, 0:C], rg[:, d, :], ALU.add).then_inc(s["v_y"], 1)

            with dve.Fori(0, ROUTED - 1) as t:
                routed(t, False)
            routed(ROUTED - 1, True)

        @block.tensor
        def _(pe):
            T = nc.tensor

            def transposed_queries(b):
                pe.wait_ge(s["v_xh"], b + 1)
                for k in range(KC):
                    for i in range(TB):
                        last = T.transpose(Sb[:, k, P * i:P * i + P], xh[:, i, P * k:P * k + P], ident[:])
                    last.then_inc(s["t_T1"], 1)

            def project_q(b):
                for m in range(KC):
                    pe.wait_ge(s["a_xT"], b * 2 + 2)
                    for k in range(KC):
                        last = T.matmul(A[m], wq[:, k, P * m:P * m + P], xT[:, k, :], start=(k == 0), stop=(k == KC - 1))
                    last.then_inc(s["t_q"], 1)

            def scores(b, i, first):
                if i == 0:
                    pe.wait_ge(s["a_qT"], b * 2 + 2)
                    pe.wait_ge(s["p_kb"], b * 2 + 2)
                    if not first:
                        pe.wait_ge(s["v_min"], b * 4)
                else:
                    pe.wait_ge(s["v_min"], b * 4 + i)
                for k in range(KC):
                    for st in range(2):
                        q = slice(64 * st, 64 * st + 64)
                        last = T.matmul(Sb[:, st, C * k:C * k + C], qT[q, k, P * i:P * i + P],
                                        kblk[q, k, :, :].rearrange("p j n -> p (j n)"), start=True, stop=True)
                last.then_inc(s["t_s"], 1)

            def probs_T(b, i, first):
                pe.wait_ge(s["a_exp"], b * 4 + i + 1)
                if i > 0:
                    pe.wait_ge(s["a_PT"], b * 8 + 2 * i)
                elif not first:
                    pe.wait_ge(s["v_x2l"], b * 2)
                for hlf in range(2):
                    for j in range(4):
                        q = 4 * hlf + j
                        last = T.transpose(A[hlf][:, P * j:P * j + P], SC[:, i % 2, P * q:P * q + P], ident[:])
                    last.then_inc(s["t_PT"], 1)

            def values(b, i, first):
                pe.wait_ge(s["a_PT"], b * 8 + 2 * i + 2)
                if i >= 2:
                    pe.wait_ge(s["v_zn"], b * 4 + i - 1)
                elif not first:
                    pe.wait_ge(s["v_zn"], b * 4 - 1 + i)
                    pe.wait_ge(s["v_slot"], b)
                for st in range(2):
                    for k in range(KC):
                        for jj in range(2):
                            q = (st * 2 + k) * 2 + jj
                            r = 4 * k + 2 * st + jj
                            last = T.matmul(Zb[i % 2][:, ZW * r:ZW * r + ZW], PT[:, q, :], vcur[:, ZW * r:ZW * r + ZW],
                                            start=True, stop=True)
                last.then_inc(s["t_z"], 1)

            def z_T(b):
                pe.wait_ge(s["v_zn"], b * 4 + 4)
                pe.wait_ge(s["a_PT"], b * 8 + 8)
                for k in range(KC):
                    for i in range(TB):
                        last = T.transpose(A[k][:, P * i:P * i + P], Zn[:, i, P * k:P * k + P], ident[:])
                    last.then_inc(s["t_ZT"], 1)

            def project_out(b):
                pe.wait_ge(s["a_ZT"], b * 2 + 2)
                for h in range(2):
                    for j in range(2):
                        i = 2 * h + j
                        for k in range(KC):
                            last = T.matmul(A[h][:, C * j:C * j + C], ZT[:, k, P * i:P * i + P], wo[:, k, :],
                                            start=(k == 0), stop=(k == KC - 1))
                    last.then_inc(s["t_wo"], 1)

            def rank(f):
                pe.wait_ge(s["v_sel"], f + 1)
                pe.wait_ge(s["v_zn"], f * 4 + 4)
                o = Zb[1]
                T.matmul(o[:, 0:TB + 1], tri[:], sel[:], start=True, stop=False)
                T.matmul(o[:, 0:TB + 1], ones[:], R[:], start=False, stop=False)
                for j in range(1, TB + 1):
                    last = T.matmul(o[:, j:TB + 1], ones[:], sel[:, 0:TB + 1 - j], start=False, stop=(j == TB))
                last.then_inc(s["t_rank"], 1)

            def ffn_in_T(f, src):
                for k in range(KC):
                    for i in range(TB):
                        last = T.transpose(A[k][:, P * i:P * i + P], src[:, i, P * k:P * k + P], ident[:])
                    last.then_inc(s["t_T2"], 1)

            def shared_in_T(f):
                pe.wait_ge(s["v_row"], f * 4 + 4)
                pe.wait_ge(s["a_qT"], f * 2 + 4)
                ffn_in_T(f, row)

            def up(f, c, routed=False):
                if c == 0:
                    pe.wait_ge(s["v_x2l"], f * 2 + 2)
                if c < 2 and routed:
                    pe.wait_ge(s["v_y"], f * 4 - 1 + c)
                if c >= 2:
                    pe.wait_ge(s["a_hf"], f * 8 + c - 1)
                n = 0
                for k in range(KC):
                    for w, xx in ((a1h, x2h), (a1h, x2l), (a1l, x2h)):
                        last = T.matmul(U[c % 2], w[:, k, P * c:P * c + P], xx[:, k, :], start=(n == 0), stop=(n == 3 * KC - 1))
                        n += 1
                last.then_inc(s["t_up"], 1)

            def down(f, d):
                if d == 0:
                    pe.wait_ge(s["v_hl"], f * 8 + 8)
                if d < 2:
                    pe.wait_ge(s["a_hf"], f * 8 + 7 + d)
                else:
                    pe.wait_ge(s["v_y"], f * 4 + d - 1)
                n = 0
                for c in range(HC):
                    for hid, w in ((hh, a2h), (hh, a2l), (hl, a2h)):
                        last = T.matmul(U[d % 2][:, 0:C], hid[:, c, P * d:P * d + P], w[:, c, :], start=(n == 0), stop=(n == 3 * HC - 1))
                        n += 1
                last.then_inc(s["t_down"], 1)

            def attention(b, first, last):
                if not first:
                    pe.wait_ge(s["v_x1"], b * 2)
                project_q(b)
                scores(b, 0, first)
                if not first:
                    f = b - 1
                    shared_in_T(f)
                scores(b, 1, first)
                if not first:
                    for c in range(3):
                        up(f, c)
                probs_T(b, 0, first)
                scores(b, 2, first)
                if not first:
                    rank(f)
                    up(f, 3)
                values(b, 0, first)
                if not first:
                    up(f, 4)
                probs_T(b, 1, first)
                scores(b, 3, first)
                if not first:
                    up(f, 5)
                values(b, 1, first)
                probs_T(b, 2, first)
                if not first:
                    up(f, 6)
                    up(f, 7)
                values(b, 2, first)
                if first:
                    pe.wait_ge(s["d_w2e"], 16)
                    pe.wait_ge(s["a_rbc"], 2)
                    for e in range(E):
                        for c in range(HC):
                            last_mm = T.matmul(U[e][:, 0:C], rbc[e][:, c, :], w2e[:, e, c, :], start=(c == 0), stop=(c == HC - 1))
                        last_mm.then_inc(s["t_const"], 1)
                probs_T(b, 3, first)
                if not first:
                    down(f, 0)
                values(b, 3, first)
                if not first:
                    down(f, 1)
                z_T(b)
                if not first:
                    down(f, 2)
                if first:
                    pe.wait_ge(s["d_wo"], 16)
                project_out(b)
                if not last:
                    pe.wait_ge(s["v_min"], b * 4 + 4)
                    transposed_queries(b + 1)
                if not first:
                    down(f, 3)

            pe.wait_ge(s["p_ident"], 4)
            pe.wait_ge(s["d_ctx"], 16)
            for k in range(KC):
                for j in range(TB):
                    last = T.transpose(A[k][:, P * j:P * j + P], ctx_nat[:, j, P * k:P * k + P], ident[:])
                last.then_inc(s["t_ctx"], 1)
            pe.wait_ge(s["d_wk"], 16)
            for m in range(KC):
                pe.wait_ge(s["v_ctxT"], 2)
                for k in range(KC):
                    last = T.matmul(Zb[m].rearrange("p (b n) -> p b n", n=KEYS), wk[:, k, P * m:P * m + P], ctxT2[:, k, :, 0, :],
                                    start=(k == 0), stop=(k == KC - 1))
                last.then_inc(s["t_k"], 1)
            pe.wait_ge(s["d_wv"], 16)
            vbank = [U[0], U[1], Sb[:, 0, :], Sb[:, 1, :]]
            for b in range(B):
                for k in range(KC):
                    last = T.matmul(vbank[b // 2][:, (b % 2) * C:(b % 2) * C + C], ctxT2[:, k, b, :, :].rearrange("p d n -> p (d n)"),
                                    wv[:, k, :], start=(k == 0), stop=(k == KC - 1))
                if b % 2 == 1:
                    last.then_inc(s["t_v"], 1)
            pe.wait_ge(s["d_wq"], 16)
            pe.wait_ge(s["v_vb"], 16)
            transposed_queries(0)
            attention(0, True, False)
            pe.wait_ge(s["v_w1l"], 1)
            pe.wait_ge(s["v_w2l"], 1)
            pe.wait_ge(s["v_crow"], 2)
            with pe.Fori(1, B - 1) as b:
                attention(b, False, False)
            attention(B - 1, False, True)
            f = B - 1
            pe.wait_ge(s["v_row"], f * 4 + 4)
            pe.wait_ge(s["v_x1"], f * 2 + 2)
            ffn_in_T(f, row)
            rank(f)
            for c in range(HC):
                up(f, c)
            pe.wait_ge(s["d_xg"], 16)
            pe.wait_ge(s["v_x2l"], f * 2 + 2)
            ffn_in_T(B, xg)
            for d in range(TB):
                down(f, d)

            def routed(t, last):
                f = t + B
                pe.wait_ge(s["v_w1l"], t + 2)
                for c in range(HC):
                    up(f, c, True)
                if not last:
                    pe.wait_ge(s["d_xg"], t * 16 + 32)
                    pe.wait_ge(s["v_x2l"], f * 2 + 2)
                    ffn_in_T(f + 1, xg)
                pe.wait_ge(s["v_w2l"], t + 2)
                for d in range(TB):
                    down(f, d)

            with pe.Fori(0, ROUTED - 1) as t:
                routed(t, False)
            routed(ROUTED - 1, True)


_INS = ["x", "ctx_1024", "mask_Bx1xSxS2_ik1",
        "L0_xattn_WQ", "L0_xattn_bQ", "L0_xattn_WK", "L0_xattn_bK", "L0_xattn_WV", "L0_xattn_bV", "L0_xattn_WO", "L0_xattn_bO",
        "L0_ffn_gate_w", "L0_ffn_w1", "L0_ffn_b1", "L0_ffn_w2", "L0_ffn_b2", "L0_ffn_sw1", "L0_ffn_sb1", "L0_ffn_sw2", "L0_ffn_sb2"]
_OUTS = [((8, 512, 256), "float32")]


def _laid_out(name, a):
    short = name.split("_", 2)[-1]
    if short in ("WQ", "WK", "WV", "WO", "sw1", "sw2"):
        return a.reshape(-1, P, a.shape[1]).transpose(1, 0, 2)
    if short in ("w1", "w2"):
        return a.reshape(a.shape[0], -1, P, a.shape[2]).transpose(0, 2, 1, 3)
    if short in ("bQ", "bK", "sb1"):
        return a.reshape(-1, P).T
    if short == "b1":
        return a.reshape(a.shape[0], -1, P).transpose(2, 0, 1)
    return a


def kernel(**inputs):
    import numpy as _np
    import concourse.bacc as _bacc
    from concourse import mybir as _mybir
    from concourse.bass_utils import run_bass_kernel_spmd as _run

    nc = _bacc.Bacc("TRN2", target_bir_lowering=False, num_devices=1)
    arrays, args = {}, []
    for name in _INS:
        a = _np.ascontiguousarray(_laid_out(name, _np.asarray(inputs[name])))
        arrays[f"in_{name}_dram"] = a
        args.append(nc.dram_tensor(f"in_{name}_dram", a.shape, _mybir.dt.from_np(a.dtype), kind="ExternalInput").ap())
    for i, (shape, dtype) in enumerate(_OUTS):
        dt = _mybir.dt.from_np(_np.dtype(dtype))
        args.append(nc.dram_tensor(f"out_{i}_dram", shape, dt, kind="ExternalOutput").ap())
    attention_and_routed_ffn(nc, *args)
    r = _run(nc, [arrays], core_ids=[0])
    got = tuple(r.results[0][f"out_{i}_dram"] for i in range(len(_OUTS)))
    return got[0]
```

```python
import concourse.bass as bass
from concourse import mybir
from contextlib import ExitStack

F32 = mybir.dt.float32
F32R = mybir.dt.float32r
BF16 = mybir.dt.bfloat16
I32 = mybir.dt.int32
ALU = mybir.AluOpType
ACT = mybir.ActivationFunctionType
AX = mybir.AxisListType

P = 128


def attention_and_routed_ffn(nc, x, ctx, mask, WQ, bQ, WK, bK, WV, bV, WO, bO,
                             gate_w, w1, b1, w2, b2, sw1, sb1, sw2, sb2, out):
    B, S, C = x.shape
    KEYS = ctx.shape[1]
    H, D = 16, 16
    E, HID = w1.shape[0], w1.shape[3]
    KC = C // P
    TB = S // P
    NT = B * TB
    HC = HID // P
    N = B * S
    SLOTS = N + S
    ROUTED = SLOTS // S
    ROW = C + 1
    PAIRS = H // 2
    ZW = 2 * (D + 1)
    NOBODY = 1 << 20
    MASKED = -1e9
    EPS = 1e-5
    NEWTON = 3
    RSTEPS = 2 + 3 * NEWTON

    xf = x.rearrange("b (p t) c -> p b (t c)", t=TB)
    outf = out.rearrange("b s c -> (b s) c")
    maskf = mask.rearrange("b a (p t) k -> p (b a) (t k)", t=TB)
    sorted_rows = nc.dram_tensor("sorted_rows", (SLOTS, ROW), F32).ap()
    resid = nc.dram_tensor("resid", (N, C), F32).ap()
    resid_v = resid.rearrange("(b p t) c -> p b (t c)", p=P, t=TB)
    sorted_v = sorted_rows.rearrange("(f p t) c -> p f (t c)", p=P, t=TB)

    es = ExitStack()
    with es:
        def sb(name, shape, dt=F32):
            return es.enter_context(nc.sbuf_tensor(name, shape, dt))

        def sem(name):
            return es.enter_context(nc.semaphore(name))

        with ExitStack() as first_life:
            cap = first_life.enter_context(nc.sbuf_tensor("cap", [P, NT, KEYS], F32))
            X = first_life.enter_context(nc.sbuf_tensor("X", [P, NT, C], F32))
        even_w = {}
        for kind in ("2l", "1h", "1l", "2h"):
            even_w[kind] = sb("even_w" + kind, [P, KC, HID] if kind[0] == "1" else [P, HC, C], F32R)
        sb("rest_of_X", [P, NT // 4, C])
        odd_w = {}
        for kind in ("2l", "1h", "1l", "2h"):
            odd_w[kind] = sb("odd_w" + kind, [P, KC, HID] if kind[0] == "1" else [P, HC, C], F32R)
        wq = sb("wq", [P, KC, C])
        wo = sb("wo", [P, KC, C])
        kT = sb("kT", [P, KC, B * KEYS])
        kblk = sb("kblk", [P, KC, 4, KEYS])
        vblk = sb("vblk", [P, B, PAIRS * ZW])
        vcur = sb("vcur", [P, PAIRS * ZW])
        xh = sb("xh", [P, TB, C])
        xT = sb("xT", [P, KC, S])
        qT = sb("qT", [P, KC, S])
        SC = sb("SC", [P, 2, H * KEYS])
        PT = sb("PT", [P, PAIRS, P])
        Zn = sb("Zn", [P, TB, C])
        ZT = xT
        row = sb("row", [P, TB, ROW])
        stage1 = sb("stage1", [P, KC, HID])
        stage2 = sb("stage2", [P, HC, C])
        x2h = sb("x2h", [P, KC, S], F32R)
        x2l = sb("x2l", [P, KC, S], F32R)
        hf = sb("hf", [P, 2, S])
        hh = sb("hh", [P, HC, S], F32R)
        hl = sb("hl", [P, HC, S], F32R)
        shared_region = sb("shared_region", [P, 2 * 4 * P * KC + TB * C])
        ctx_nat = shared_region[:, 0:TB * C].rearrange("p (j c) -> p j c", c=C)
        ctxT2 = shared_region[:, TB * C:TB * C + KC * B * 2 * KEYS].rearrange(
            "p (k b d n) -> p k b d n", k=KC, b=B, d=2)
        wk = stage1[:, 0, 0:KC * C].rearrange("p (k c) -> p k c", k=KC)
        wv = stage1[:, 1, 0:KC * C].rearrange("p (k c) -> p k c", k=KC)
        rg = shared_region[:, 0:TB * C].rearrange("p (j c) -> p j c", c=C)
        xg = shared_region[:, TB * C:TB * C + TB * ROW].rearrange("p (j c) -> p j c", c=ROW)
        bo_b = sb("bo_b", [P, C])
        bv_b = sb("bv_b", [P, C])
        gw_b = sb("gw_b", [P, E, C])
        crow = sb("crow", [P, E, C])
        crow_cur = sb("crow_cur", [P, C])
        bq_c = sb("bq_c", [P, KC])
        bk_c = sb("bk_c", [P, KC])
        b1_c = sb("b1_c", [P, E, HC])
        b1_cur = sb("b1_cur", [P, HC])
        rb1 = sb("rb1", [P, E, HC])
        ident = sb("ident", [P, P])
        tri = sb("tri", [P, P], BF16)
        ones = sb("ones", [P, P], BF16)
        dmask = sb("dmask", [P, 4])
        tok_i = sb("tok_i", [P, NT], I32)
        ord_i = sb("ord_i", [P, NT], I32)
        tok_f = sb("tok_f", [P, NT])
        tok_r = sb("tok_r", [P, NT])
        tile_i = sb("tile_i", [P, ROUTED], I32)
        tile_f = sb("tile_f", [P, ROUTED])
        exp_f = sb("exp_f", [P, ROUTED])
        exp_i = sb("exp_i", [P, ROUTED], I32)
        n0 = sb("n0", [P, 1])
        fill = sb("fill", [P, ROW])
        stA, stB = sb("stA", [P, TB, 6]), sb("stB", [P, TB, 6])
        mvA, mvB = sb("mvA", [P, TB, 2]), sb("mvB", [P, TB, 2])
        rsA, rsB = sb("rsA", [P, TB]), sb("rsB", [P, TB])
        rv, rt = sb("rv", [P, TB]), sb("rt", [P, TB])
        mx = sb("mx", [P, 2, H])
        rec = sb("rec", [P, 2, H])
        gsc = sb("gsc", [P, TB, E])
        sel = sb("sel", [P, TB + 1], BF16)
        R = sb("R", [P, TB + 1], BF16)

        rsum = sb("rsum", [P, 1])
        slotA, slotB = sb("slotA", [P, TB]), sb("slotB", [P, TB])
        slot_i = sb("slot_i", [P, TB], I32)
        ids = sb("ids", [P, TB], I32)
        nids = sb("nids", [P, TB], I32)

        ps = es.enter_context(nc.psum_tensor("ps", [P, 8, 512], F32))
        U = [ps[:, 0, :], ps[:, 1, :]]
        Sb = ps[:, 2:4, :]
        A = [ps[:, 4, :], ps[:, 5, :]]
        Zb = [ps[:, 6, :], ps[:, 7, :]]

        names = """d_x d_ctx d_wk d_wv d_wq d_wo d_mask d_vec d_kvb d_w2e d_stage1 d_stage2 d_b1 d_fill d_res
            d_scat d_xg d_rg d_crow d_out
            p_ident p_dmask p_tabs p_fill p_vz p_kb p_xb p_sub p_rowid p_ids p_nid p_rgc p_sel0
            v_ctxT v_kT v_vb v_tok v_tokr v_cvec v_cap v_rb1 v_crow0 v_crow v_st1 v_mv1 v_rs1 v_xh v_min v_max v_x2l v_hh v_hl
            v_rec v_zn v_y v_x1 v_st2 v_mv2 v_rs2 v_row v_gate v_sel v_sa v_sb v_slot v_rsum v_R v_n0 v_exp
            v_expi v_w1l v_w2l v_rbx
            a_rbc a_xT a_qT a_exp a_PT a_ZT a_x2h a_hf a_w1h a_w2h
            t_ctx t_k t_v t_const t_T1 t_q t_s t_PT t_z t_ZT t_wo t_rank t_T2 t_up t_down""".split()
        s = {n: sem(n) for n in names}

        routed_down = Zb + U

        def other(weights):
            return odd_w if weights is even_w else even_w

        def up_bank(c, routed):
            return (c + 2) % 4 if routed else c % 2

        def halves(bank):
            return bank.rearrange("p (j c) -> p j c", c=C)

        rbc = [hf[:, :, :].rearrange("p a n -> p (a n)").rearrange("p (c m) -> p c m", m=P),
               row[:, :, :].rearrange("p a n -> p (a n)")[:, 0:HC * P].rearrange("p (c m) -> p c m", m=P)]
        w2e = X[:, NT // 2:NT, :].rearrange("p (e j) c -> p e j c", e=E)

        block = es.enter_context(nc.Block())

        @block.sync
        def _(sp):
            sp.dma_start(ctx_nat, ctx.rearrange("b k c -> (b k) c").rearrange("(j p) c -> p j c", p=P)).then_inc(s["d_ctx"], 16)
            sp.dma_start(X[:, 0:TB, :].rearrange("p t c -> p (t c)"), xf[:, 0, :]).then_inc(s["d_x"], 16)
            sp.dma_start(wk, WK).then_inc(s["d_wk"], 16)
            sp.dma_start(wv, WV).then_inc(s["d_wv"], 16)
            sp.dma_start(wq[:], WQ).then_inc(s["d_wq"], 16)
            sp.dma_start(cap[:, :, :].bitcast(I32).rearrange("p (b t) k -> p b (t k)", t=TB), maskf).then_inc(s["d_mask"], 16)
            sp.dma_start(w2e, w2.rearrange("e p j c -> p e j c")).then_inc(s["d_w2e"], 16)
            sp.dma_start(wo[:], WO).then_inc(s["d_wo"], 16)
            sp.wait_ge(s["d_x"], 16)
            sp.dma_start(X[:, TB:2 * TB, :].rearrange("p t c -> p (t c)"), xf[:, 1, :]).then_inc(s["d_x"], 16)
            sp.wait_ge(s["t_v"], 4)
            sp.dma_start(stage1[:], sw1).then_inc(s["d_stage1"], 16)
            sp.dma_start(stage2[:], sw2).then_inc(s["d_stage2"], 16)
            for b in range(2, B // 2):
                sp.wait_ge(s["d_x"], 16 * b)
                sp.dma_start(X[:, TB * b:TB * b + TB, :].rearrange("p t c -> p (t c)"), xf[:, b, :]).then_inc(s["d_x"], 16)
            sp.wait_ge(s["p_fill"], 2)
            sp.dma_start(sorted_rows.rearrange("(p r) c -> p r c", p=P),
                         fill[:, :].unsqueeze(1).broadcast_to([P, SLOTS // P, ROW])).then_inc(s["d_fill"], 16)
            sp.wait_ge(s["t_const"], 2)
            for b in range(B // 2, B):
                sp.wait_ge(s["d_x"], 16 * b)
                sp.dma_start(X[:, TB * b:TB * b + TB, :].rearrange("p t c -> p (t c)"), xf[:, b, :]).then_inc(s["d_x"], 16)
            def resid_out(b):
                sp.wait_ge(s["v_y"], b * 4 + 4)
                sp.dma_start(resid_v[:, bass.ds(b, 1), :].rearrange("p b n -> p (b n)"),
                             X[:, bass.ds(b * TB, TB), :].rearrange("p t c -> p (t c)")).then_inc(s["d_res"], 16)

            def routed_in(t, first):
                e = sp.value_load(exp_i[0:1, bass.ds(t, 1)], min_val=0, max_val=E - 1)
                sp.wait_ge(s["v_w1l"], t + 1)
                sp.dma_start(stage1[:], w1[bass.ds(e, 1), :, :, :].rearrange("e p k n -> (e p) k n")).then_inc(s["d_stage1"], 16)
                sp.wait_ge(s["v_w2l"], t + 1)
                sp.dma_start(stage2[:], w2[bass.ds(e, 1), :, :, :].rearrange("e p j c -> (e p) j c")).then_inc(s["d_stage2"], 16)
                if first:
                    sp.wait_ge(s["d_scat"], 64 * B)
                else:
                    sp.wait_ge(s["p_nid"], t)
                    sp.wait_ge(s["t_T2"], t * 2 + 2 * B)
                sp.dma_start(xg.rearrange("p j c -> p (j c)"), sorted_v[:, bass.ds(t, 1), :].rearrange("p f n -> p (f n)")).then_inc(s["d_xg"], 16)
                sp.wait_ge(s["a_hf"], t * 8 + 8 * B)
                sp.dma_start(b1_cur[:], b1_c[:, bass.ds(e, 1), :].rearrange("p e j -> p (e j)")).then_inc(s["d_b1"], 16)
                sp.wait_ge(s["p_rgc"], t + 2)
                sp.dma_start(crow_cur[:], crow[:, bass.ds(e, 1), :].rearrange("p e c -> p (e c)")).then_inc(s["d_crow"], 16)

            with sp.Fori(0, B - 1) as b:
                resid_out(b)
            sp.wait_ge(s["v_expi"], 1)
            routed_in(0, True)
            resid_out(B - 1)
            with sp.Fori(1, ROUTED) as t:
                routed_in(t, False)
            sp.wait_ge(s["d_res"], 16 * B)
            sp.wait_ge(s["d_out"], 64 * ROUTED)

        @block.gpsimd
        def _(pool):
            g = nc.gpsimd
            g.memset(ones[:], 1.0).then_inc(s["p_ident"], 1)
            g.memset(dmask[:], 1.0).then_inc(s["p_ident"], 1)
            pool.wait_ge(s["p_ident"], 2)
            g.affine_select(out=ident[:], in_=ones[:], compare_op=ALU.is_equal, fill=0.0, base=0,
                            pattern=[[-1, P]], channel_multiplier=1).then_inc(s["p_ident"], 1)
            g.affine_select(out=tri[:], in_=ones[:], compare_op=ALU.is_gt, fill=0.0, base=0,
                            pattern=[[1, P]], channel_multiplier=-1).then_inc(s["p_ident"], 1)
            pool.wait_ge(s["p_ident"], 4)
            for r in range(2):
                g.affine_select(out=dmask[64 * r:64 * r + 64, :], in_=dmask[64 * r:64 * r + 64, :], compare_op=ALU.is_ge,
                                fill=0.0, base=0, pattern=[[-D, 4]], channel_multiplier=1).then_inc(s["p_dmask"], 1)
            pool.wait_ge(s["p_dmask"], 2)
            for r in range(2):
                g.affine_select(out=dmask[64 * r:64 * r + 64, :], in_=dmask[64 * r:64 * r + 64, :], compare_op=ALU.is_ge,
                                fill=0.0, base=D - 1, pattern=[[D, 4]], channel_multiplier=-1).then_inc(s["p_dmask"], 1)
            pool.wait_ge(s["p_dmask"], 4)
            g.memset(vblk[:], 0.0).then_inc(s["p_vz"], 1)
            pool.wait_ge(s["p_vz"], 1)
            vv = vblk[:, :, :].rearrange("p b (r w) -> p b r w", w=ZW)
            g.memset(vv[0:KEYS, :, :, D:D + 1], 1.0).then_inc(s["p_vz"], 1)
            g.memset(vv[KEYS:P, :, :, ZW - 1:ZW], 1.0).then_inc(s["p_vz"], 1)
            pool.wait_ge(s["p_vz"], 3)
            g.iota(tok_i[:], pattern=[[S, B], [1, TB]], base=0, channel_multiplier=TB).then_inc(s["p_tabs"], 1)
            g.iota(ord_i[:], pattern=[[P, NT]], base=0, channel_multiplier=1).then_inc(s["p_tabs"], 1)
            g.iota(tile_i[:], pattern=[[S, ROUTED]], base=0, channel_multiplier=0).then_inc(s["p_tabs"], 1)
            g.memset(sel[:], 0.0).then_inc(s["p_sel0"], 1)
            g.memset(R[:], 0.0).then_inc(s["p_sel0"], 1)
            g.memset(fill[:, 0:C], 0.0).then_inc(s["p_fill"], 1)
            g.memset(fill[:, C:ROW].bitcast(I32), NOBODY).then_inc(s["p_fill"], 1)

            def keys_of(b):
                pool.wait_ge(s["v_kT"], 2)
                pool.wait_ge(s["p_dmask"], 4)
                pool.wait_ge(s["v_vb"], 16)
                pool.wait_ge(s["p_vz"], 3)
                pool.wait_ge(s["d_x"], b * 16 + 16)
                pool.wait_ge(s["d_vec"], 6 * 16)
                pool.wait_ge(s["v_xh"], b + 1)
                g.tensor_tensor(X[:, bass.ds(b * TB, TB), :], X[:, bass.ds(b * TB, TB), :],
                                bo_b[:, :].unsqueeze(1).broadcast_to([P, TB, C]), ALU.add).then_inc(s["p_xb"], 1)

            def keys_build(b, first):
                if not first:
                    pool.wait_ge(s["t_s"], b * 4)
                    pool.wait_ge(s["t_z"], b * 4)
                g.tensor_tensor(kblk[:], kT[:, :, bass.ds(b * KEYS, KEYS)].unsqueeze(2).broadcast_to([P, KC, 4, KEYS]),
                                dmask[:, :].unsqueeze(1).unsqueeze(3).broadcast_to([P, KC, 4, KEYS]),
                                ALU.mult).then_inc(s["p_kb"], 1)
                g.tensor_copy(vcur[:], vblk[:, bass.ds(b, 1), :].rearrange("p b w -> p (b w)")).then_inc(s["p_kb"], 1)

            def subtract_max(b, i):
                pool.wait_ge(s["v_max"], b * 4 + i + 1)
                sc = SC[:, i % 2, :].rearrange("p (h k) -> p h k", k=KEYS)
                g.tensor_tensor(sc, sc, mx[:, i % 2, :].unsqueeze(2).broadcast_to([P, H, KEYS]),
                                ALU.subtract).then_inc(s["p_sub"], 1)

            def scatter(f):
                pool.wait_ge(s["v_row"], f * 4 + 4)
                g.tensor_copy(row[:, :, C].bitcast(I32), tok_i[:, bass.ds(f * TB, TB)]).then_inc(s["p_rowid"], 1)
                pool.wait_ge(s["d_fill"], 16)
                pool.wait_ge(s["p_rowid"], f + 1)
                pool.wait_ge(s["v_slot"], f + 1)
                for j in range(TB):
                    g.indirect_dma_start(out=sorted_rows, out_offset=bass.IndirectOffsetOnAxis(ap=slot_i[:, j:j + 1], axis=0),
                                         in_=row[:, j, :], in_offset=None).then_inc(s["d_scat"], 16)

            def attention(b, first):
                keys_build(b, first)
                keys_of(b)
                subtract_max(b, 0)
                subtract_max(b, 1)
                subtract_max(b, 2)
                if not first:
                    scatter(b - 1)
                subtract_max(b, 3)

            pool.wait_ge(s["v_kT"], 2)
            pool.wait_ge(s["p_dmask"], 4)
            pool.wait_ge(s["v_vb"], 16)
            pool.wait_ge(s["p_vz"], 3)
            attention(0, True)
            with pool.Fori(1, B) as b:
                attention(b, False)
            scatter(B - 1)
            pool.wait_ge(s["t_ctx"], 2)
            pool.wait_ge(s["t_v"], 4)
            g.memset(rg[:, 0:2, :], 0.0).then_inc(s["p_rgc"], 1)
            g.memset(rg[:, 2:4, :], 0.0).then_inc(s["p_rgc"], 1)

            def numbers(t):
                pool.compute_val(t * 16 + 16)
                pool.wait_ge(s["d_xg"], 16)
                pool.wait_ge(s["d_xg"], t * 16 + 16)
                g.tensor_copy(nids[:], xg[:, :, C].bitcast(I32)).then_inc(s["p_nid"], 1)

            def routed(t, last):
                pool.compute_val(t + 1)
                pool.wait_ge(s["p_nid"], 1)
                pool.wait_ge(s["p_nid"], t + 1)
                g.tensor_copy(ids[:], nids[:]).then_inc(s["p_ids"], 1)
                pool.compute_val(t + 1)
                pool.wait_ge(s["d_res"], 16 * B)
                pool.wait_ge(s["p_rgc"], 2)
                pool.wait_ge(s["p_ids"], t + 1)
                for j in range(TB):
                    g.indirect_dma_start(out=rg[:, j, :], out_offset=None, in_=resid,
                                         in_offset=bass.IndirectOffsetOnAxis(ap=ids[:, j:j + 1], axis=0),
                                         bounds_check=N - 1, oob_is_err=False).then_inc(s["d_rg"], 16)
                pool.wait_ge(s["d_rg"], t * 64 + 64)
                pool.wait_ge(s["d_crow"], t * 16 + 16)
                g.tensor_tensor(rg, rg, crow_cur[:, :].unsqueeze(1).broadcast_to([P, TB, C]), ALU.add).then_inc(s["p_rgc"], 1)
                if not last:
                    numbers(t + 1)
                for j in range(TB):
                    pool.compute_val(t * 4 + (4 * B + j + 1))
                    pool.wait_ge(s["v_y"], 4 * B)
                    pool.wait_ge(s["v_y"], t * 4 + (4 * B + j + 1))
                    g.indirect_dma_start(out=outf, out_offset=bass.IndirectOffsetOnAxis(ap=ids[:, j:j + 1], axis=0),
                                         in_=rg[:, j, :], in_offset=None,
                                         bounds_check=N - 1, oob_is_err=False).then_inc(s["d_out"], 16)
                pool.wait_ge(s["d_out"], t * 64 + 64)

            numbers(0)
            with pool.Fori(0, ROUTED - 1) as t:
                routed(t, False)
            routed(ROUTED - 1, True)

        @block.scalar
        def _(act):
            a = nc.scalar
            act.dma_start(bk_c[:], bK).then_inc(s["d_kvb"], 16)
            act.dma_start(bv_b[:], bV.partition_broadcast(P)).then_inc(s["d_kvb"], 16)
            act.dma_start(bq_c[:], bQ).then_inc(s["d_vec"], 16)
            act.dma_start(b1_c[:], b1).then_inc(s["d_vec"], 16)
            act.dma_start(bo_b[:], bO.partition_broadcast(P)).then_inc(s["d_vec"], 16)
            act.dma_start(gw_b[:], gate_w.partition_broadcast(P)).then_inc(s["d_vec"], 16)
            act.dma_start(crow[:], b2.partition_broadcast(P)).then_inc(s["d_vec"], 16)
            act.dma_start(crow_cur[:], sb2.partition_broadcast(P)).then_inc(s["d_vec"], 16)
            act.dma_start(b1_cur[:], sb1).then_inc(s["d_b1"], 16)

            def queries_T(b):
                for k in range(KC):
                    act.wait_ge(s["t_T1"], b * 2 + k + 1)
                    act.wait_ge(s["t_wo"], b * 2)
                    a.activation(xT[:, k, :], Sb[:, k, :], ACT.Copy).then_inc(s["a_xT"], 1)

            def project_q(b):
                for m in range(KC):
                    act.wait_ge(s["t_q"], b * 2 + m + 1)
                    a.activation(qT[:, m, :], A[m], ACT.Identity, bias=bq_c[:, m:m + 1]).then_inc(s["a_qT"], 1)

            def expo(b, i):
                act.wait_ge(s["p_sub"], b * 4 + i + 1)
                a.activation(SC[:, i % 2, :], SC[:, i % 2, :], ACT.Exp).then_inc(s["a_exp"], 1)

            def probs_T(b, i):
                for hlf in range(2):
                    act.wait_ge(s["t_PT"], b * 8 + 2 * i + hlf + 1)
                    if i > 0 and hlf == 0:
                        act.wait_ge(s["t_z"], b * 4 + i)
                    a.activation(PT[:, 4 * hlf:4 * hlf + 4, :].rearrange("p a n -> p (a n)"), A[hlf], ACT.Copy).then_inc(s["a_PT"], 1)

            def z_T(b):
                for k in range(KC):
                    act.wait_ge(s["t_ZT"], b * 2 + k + 1)
                    a.activation(ZT[:, k, :], A[k], ACT.Copy).then_inc(s["a_ZT"], 1)

            def ffn_in_high(f, banks=Zb):
                for k in range(KC):
                    act.wait_ge(s["t_T2"], f * 2 + k + 1)
                    a.activation(x2h[:, k, :], banks[k], ACT.Copy).then_inc(s["a_x2h"], 1)

            def split_high(kind, at):
                a.activation(at[kind + "h"][:], (stage1 if kind == "1" else stage2)[:], ACT.Copy).then_inc(s[f"a_w{kind}h"], 1)

            def hidden(f, c, routed=False):
                act.wait_ge(s["t_up"], f * 8 + c + 1)
                if c >= 2:
                    act.wait_ge(s["v_hl"], f * 8 + c - 1)
                a.activation(hf[:, c % 2, :], ps[:, up_bank(c, routed), :], ACT.Relu, bias=b1_cur[:, c:c + 1]).then_inc(s["a_hf"], 1)

            def attention(b, first, last):
                project_q(b)
                if first:
                    act.wait_ge(s["v_rb1"], 1)
                    for e in range(E):
                        a.activation(rbc[e], rb1[:, e, :].unsqueeze(2).broadcast_to([P, HC, P]), ACT.Copy).then_inc(s["a_rbc"], 1)
                else:
                    f = b - 1
                    ffn_in_high(f)
                    hidden(f, 0)
                    hidden(f, 1)
                expo(b, 0)
                if not first:
                    hidden(f, 2)
                probs_T(b, 0)
                expo(b, 1)
                if not first:
                    hidden(f, 3)
                    hidden(f, 4)
                probs_T(b, 1)
                expo(b, 2)
                if first:
                    act.wait_ge(s["d_stage1"], 16)
                    split_high("1", odd_w)
                else:
                    hidden(f, 5)
                probs_T(b, 2)
                if not first:
                    hidden(f, 6)
                expo(b, 3)
                if first:
                    act.wait_ge(s["d_stage2"], 16)
                    split_high("2", odd_w)
                else:
                    hidden(f, 7)
                probs_T(b, 3)
                z_T(b)
                if not last:
                    queries_T(b + 1)

            act.wait_ge(s["d_vec"], 6 * 16)
            for k in range(KC):
                act.wait_ge(s["t_T1"], k + 1)
                a.activation(xT[:, k, :], Sb[:, k, :], ACT.Copy).then_inc(s["a_xT"], 1)
            attention(0, True, False)
            act.wait_ge(s["d_b1"], 16)
            with act.Fori(1, B - 1) as b:
                attention(b, False, False)
            attention(B - 1, False, True)
            ffn_in_high(B - 1)
            for c in range(HC):
                hidden(B - 1, c)

            def prepare(t, at):
                ffn_in_high(t + B, A)
                act.wait_ge(s["d_stage1"], t * 16 + 32)
                split_high("1", at)
                act.wait_ge(s["d_stage2"], t * 16 + 32)
                split_high("2", at)

            def routed(t, at, last):
                act.wait_ge(s["d_b1"], t * 16 + 32)
                for c in range(HC):
                    hidden(t + B, c, True)
                if not last:
                    prepare(t + 1, other(at))

            act.wait_ge(s["d_res"], 16 * (B - 2))
            prepare(0, even_w)
            with act.Fori(0, ROUTED // 2) as u:
                routed(u * 2, even_w, False)
                routed(u * 2 + 1, odd_w, False)
            routed(ROUTED - 1, even_w, True)

        @block.vector
        def _(dve):
            v = nc.vector

            def inverse_root(b, mv, rs, done):
                v.tensor_scalar(rv[:], mv[:, :, 1], EPS, None, ALU.add).then_inc(done, 1)
                dve.wait_ge(done, b * RSTEPS + 1)
                v.tensor_scalar(rs[:, :].bitcast(I32), rv[:, :].bitcast(I32), -0.5, float(0x5F3759DF),
                                ALU.mult, ALU.add).then_inc(done, 1)
                dve.wait_ge(done, b * RSTEPS + 2)
                for k in range(NEWTON):
                    v.tensor_tensor(rt[:], rs[:], rs[:], ALU.mult).then_inc(done, 1)
                    dve.wait_ge(done, b * RSTEPS + 3 * k + 3)
                    v.scalar_tensor_tensor(out=rt[:], in0=rt[:], scalar=-0.5, in1=rv[:], op0=ALU.mult, op1=ALU.mult).then_inc(done, 1)
                    dve.wait_ge(done, b * RSTEPS + 3 * k + 4)
                    v.scalar_tensor_tensor(out=rs[:], in0=rt[:], scalar=1.5, in1=rs[:], op0=ALU.add, op1=ALU.mult).then_inc(done, 1)
                    dve.wait_ge(done, b * RSTEPS + 3 * k + 5)

            def norm1(b):
                dve.wait_ge(s["d_x"], 16)
                dve.wait_ge(s["d_x"], b * 16 + 16)
                for i in range(TB):
                    last = v.bn_stats(stA[:, i, :], X[:, bass.ds(b * TB + i, 1), :].rearrange("p a c -> p (a c)"))
                last.then_inc(s["v_st1"], 1)
                dve.compute_val(b + 1)
                dve.wait_ge(s["v_st1"], 1)
                dve.wait_ge(s["v_st1"], b + 1)
                for i in range(TB):
                    last = v.bn_aggr(mvA[:, i, :], stA[:, i, :])
                last.then_inc(s["v_mv1"], 1)
                dve.wait_ge(s["v_mv1"], b + 1)
                inverse_root(b, mvA, rsA, s["v_rs1"])
                if not isinstance(b, int) or b > 0:
                    dve.wait_ge(s["t_T1"], b * 2)
                for i in range(TB):
                    last = v.tensor_scalar(xh[:, i, :], X[:, bass.ds(b * TB + i, 1), :].rearrange("p a c -> p (a c)"),
                                           mvA[:, i, 0:1], rsA[:, i:i + 1], ALU.subtract, ALU.mult)
                last.then_inc(s["v_xh"], 1)

            def masked_max(b, i, first):
                dve.wait_ge(s["t_s"], b * 4 + i + 1)
                if i >= 2:
                    dve.wait_ge(s["t_PT"], b * 8 + 2 * i - 2)
                elif not first:
                    dve.wait_ge(s["t_PT"], b * 8 - 4 + 2 * i)
                sc = SC[:, i % 2, :].rearrange("p (h k) -> p h k", k=KEYS)
                v.tensor_tensor(sc, Sb.rearrange("p s (h k) -> p (s h) k", k=KEYS),
                                cap[:, bass.ds(b * TB + i, 1), :].broadcast_to([P, H, KEYS]), ALU.min).then_inc(s["v_min"], 1)
                dve.wait_ge(s["v_min"], b * 4 + i + 1)
                v.tensor_reduce(mx[:, i % 2, :], sc, AX.X, ALU.max).then_inc(s["v_max"], 1)

            def normalise(b, i):
                dve.wait_ge(s["t_z"], b * 4 + i + 1)
                z = Zb[i % 2][:, 0:H * (D + 1)].rearrange("p (h w) -> p h w", w=D + 1)
                v.reciprocal(rec[:, i % 2, :], z[:, :, D]).then_inc(s["v_rec"], 1)
                dve.wait_ge(s["v_rec"], b * 4 + i + 1)
                v.tensor_tensor(Zn[:, i, :].rearrange("p (h d) -> p h d", d=D), z[:, :, 0:D],
                                rec[:, i % 2, :].unsqueeze(2).broadcast_to([P, H, D]), ALU.mult).then_inc(s["v_zn"], 1)

            def attended(b):
                dve.wait_ge(s["p_xb"], b + 1)
                for h in range(2):
                    dve.wait_ge(s["t_wo"], b * 2 + h + 1)
                    xs = X[:, bass.ds(b * TB + 2 * h, 2), :]
                    v.tensor_tensor(xs, halves(A[h]), xs, ALU.add).then_inc(s["v_x1"], 1)

            def norm2(b, first):
                dve.wait_ge(s["v_x1"], 2)
                dve.wait_ge(s["v_x1"], b * 2 + 2)
                for i in range(TB):
                    last = v.bn_stats(stB[:, i, :], X[:, bass.ds(b * TB + i, 1), :].rearrange("p a c -> p (a c)"))
                last.then_inc(s["v_st2"], 1)
                dve.compute_val(b + 1)
                dve.wait_ge(s["v_st2"], 1)
                dve.wait_ge(s["v_st2"], b + 1)
                for i in range(TB):
                    last = v.bn_aggr(mvB[:, i, :], stB[:, i, :])
                last.then_inc(s["v_mv2"], 1)
                dve.wait_ge(s["v_mv2"], b + 1)
                inverse_root(b, mvB, rsB, s["v_rs2"])
                if not first:
                    dve.wait_ge(s["d_scat"], b * 64)
                    dve.wait_ge(s["t_T2"], b * 2)
                for i in range(TB):
                    v.tensor_scalar(row[:, i, 0:C], X[:, bass.ds(b * TB + i, 1), :].rearrange("p a c -> p (a c)"),
                                    mvB[:, i, 0:1], rsB[:, i:i + 1], ALU.subtract, ALU.mult).then_inc(s["v_row"], 1)

            def gate(b, e):
                dve.wait_ge(s["v_row"], b * 4 + 4)
                for i in range(TB):
                    if e > 0:
                        dve.wait_ge(s["v_gate"], b * 8 + i + 1)
                    v.tensor_tensor_reduce(out=Zn[:, i, :], in0=row[:, i, 0:C], in1=gw_b[:, e, :], scale=1.0, scalar=0.0,
                                           op0=ALU.mult, op1=ALU.add, accum_out=gsc[:, i, e:e + 1]).then_inc(s["v_gate"], 1)

            def choose(b):
                dve.wait_ge(s["v_gate"], b * 8 + 8)
                v.tensor_tensor(sel[:, 0:TB], gsc[:, :, 1], gsc[:, :, 0], ALU.is_gt).then_inc(s["v_sel"], 1)

            def slots(f):
                dve.wait_ge(s["t_rank"], f + 1)
                r = Zb[1][:, 0:TB]
                v.scalar_tensor_tensor(out=slotA[:], in0=r, scalar=-1.0, in1=tok_f[:, bass.ds(f * TB, TB)],
                                       op0=ALU.mult, op1=ALU.add).then_inc(s["v_sa"], 1)
                v.tensor_tensor(slotB[:], sel[:, 0:TB], tok_r[:, bass.ds(f * TB, TB)], ALU.mult).then_inc(s["v_sb"], 1)
                v.tensor_reduce(rsum[:], sel[:, 0:TB], AX.X, ALU.add).then_inc(s["v_rsum"], 1)
                dve.wait_ge(s["v_sa"], f + 1)
                dve.wait_ge(s["v_sb"], f + 1)
                v.tensor_tensor(slot_i[:], slotA[:], slotB[:], ALU.add).then_inc(s["v_slot"], 1)
                dve.wait_ge(s["v_rsum"], f + 1)
                v.tensor_tensor(R[:], R[:], rsum[:, :].broadcast_to([P, TB + 1]), ALU.add).then_inc(s["v_R"], 1)

            def ffn_in_low(f, banks=Zb):
                for k in range(KC):
                    dve.wait_ge(s["a_x2h"], f * 2 + k + 1)
                    v.tensor_tensor(x2l[:, k, :], banks[k], x2h[:, k, :].bitcast(F32), ALU.subtract).then_inc(s["v_x2l"], 1)

            def hidden_split(f, c):
                dve.wait_ge(s["a_hf"], f * 8 + c + 1)
                v.tensor_copy(hh[:, c, :], hf[:, c % 2, :]).then_inc(s["v_hh"], 1)
                dve.wait_ge(s["v_hh"], f * 8 + c + 1)
                v.tensor_tensor(hl[:, c, :], hf[:, c % 2, :], hh[:, c, :].bitcast(F32), ALU.subtract).then_inc(s["v_hl"], 1)

            def shared_out(f, d):
                dve.wait_ge(s["t_down"], f * 4 + d + 1)
                xs = X[:, bass.ds(f * TB + d, 1), :].rearrange("p a c -> p (a c)")
                v.tensor_tensor(xs, U[d % 2][:, 0:C], xs, ALU.add).then_inc(s["v_y"], 1)

            def split_low(kind, at, splits):
                dve.wait_ge(s[f"a_w{kind}h"], splits)
                v.tensor_tensor(at[kind + "l"][:], (stage1 if kind == "1" else stage2)[:], at[kind + "h"][:, :, :].bitcast(F32),
                                ALU.subtract).then_inc(s[f"v_w{kind}l"], 1)

            def attention(b, first, last):
                f = b - 1
                if not first:
                    ffn_in_low(f)
                masked_max(b, 0, first)
                if not first:
                    hidden_split(f, 0)
                    hidden_split(f, 1)
                masked_max(b, 1, first)
                if not first:
                    gate(f, 0)
                    hidden_split(f, 2)
                    gate(f, 1)
                    choose(f)
                masked_max(b, 2, first)
                normalise(b, 0)
                if not first:
                    hidden_split(f, 3)
                    slots(f)
                    hidden_split(f, 4)
                masked_max(b, 3, first)
                if first:
                    split_low("1", odd_w, 1)
                else:
                    hidden_split(f, 5)
                normalise(b, 1)
                if first:
                    split_low("2", odd_w, 1)
                    for e in range(E):
                        dve.wait_ge(s["t_const"], e + 1)
                        v.tensor_tensor(crow[:, 1 - e, :], U[e][:, 0:C], crow_cur[:], ALU.add).then_inc(s["v_crow"], 1)
                else:
                    hidden_split(f, 6)
                    hidden_split(f, 7)
                normalise(b, 2)
                if not last:
                    norm1(b + 1)
                normalise(b, 3)
                if not first:
                    shared_out(f, 0)
                    shared_out(f, 1)
                    shared_out(f, 2)
                attended(b)
                norm2(b, first)
                if not first:
                    shared_out(f, 3)

            for k in range(KC):
                dve.wait_ge(s["t_ctx"], k + 1)
                src = A[k].rearrange("p (b n) -> p b n", n=KEYS)
                for d in range(2):
                    last = v.tensor_copy(ctxT2[:, k, :, d, :], src)
                last.then_inc(s["v_ctxT"], 1)
            norm1(0)
            dve.wait_ge(s["d_mask"], 16)
            v.tensor_scalar(cap[:], cap[:, :, :].bitcast(I32), 0.0, -2e30, ALU.is_equal, ALU.mult).then_inc(s["v_cap"], 1)
            dve.wait_ge(s["v_cap"], 1)
            v.tensor_scalar(cap[:], cap[:], 1e30, MASKED, ALU.add, ALU.max).then_inc(s["v_cap"], 1)
            dve.wait_ge(s["d_kvb"], 2 * 16)
            for m in range(KC):
                dve.wait_ge(s["t_k"], m + 1)
                v.tensor_scalar(kT[:, m, :], Zb[m], bk_c[:, m:m + 1], 0.25, ALU.add, ALU.mult).then_inc(s["v_kT"], 1)
            dve.wait_ge(s["p_vz"], 3)
            vb = vblk[:, :, :].rearrange("p b (r o w) -> p b r o w", o=2, w=D + 1)
            vbank = A + U
            for b in range(B):
                dve.wait_ge(s["t_v"], b // 2 + 1)
                src = vbank[b // 2][:, (b % 2) * C:(b % 2) * C + C].rearrange("p (r o d) -> p r o d", o=2, d=D)
                bias = bv_b[:, :].rearrange("p (r o d) -> p r o d", o=2, d=D)
                for o in range(2):
                    q = slice(64 * o, 64 * o + 64)
                    v.tensor_tensor(vb[q, b, :, o, 0:D], src[q, :, o, :], bias[q, :, o, :], ALU.add).then_inc(s["v_vb"], 1)
            dve.wait_ge(s["d_vec"], 6 * 16)
            v.tensor_scalar(rb1[:], b1_c[:], 0.0, None, ALU.max).then_inc(s["v_rb1"], 1)
            dve.wait_ge(s["p_tabs"], 3)
            v.tensor_copy(tok_f[:], ord_i[:]).then_inc(s["v_tok"], 1)
            v.tensor_copy(tile_f[:], tile_i[:])
            dve.wait_ge(s["v_tok"], 1)
            v.tensor_scalar(tok_r[:], tok_f[:], -1.0, float(SLOTS - 1), ALU.mult, ALU.add).then_inc(s["v_tokr"], 1)
            v.tensor_tensor(crow_cur[:], crow_cur[:], crow[:, 0, :], ALU.add).then_inc(s["v_cvec"], 1)
            dve.wait_ge(s["v_cvec"], 1)
            v.tensor_tensor(crow_cur[:], crow_cur[:], crow[:, 1, :], ALU.add).then_inc(s["v_cvec"], 1)
            dve.wait_ge(s["v_cvec"], 2)
            dve.wait_ge(s["v_tokr"], 1)
            dve.wait_ge(s["v_cap"], 2)
            dve.wait_ge(s["p_sel0"], 2)
            attention(0, True, False)
            with dve.Fori(1, B - 1) as b:
                attention(b, False, False)
            attention(B - 1, False, True)
            ffn_in_low(B - 1)
            gate(B - 1, 0)
            gate(B - 1, 1)
            choose(B - 1)
            slots(B - 1)
            v.tensor_scalar(n0[:], Zb[1][:, TB:TB + 1], -1.0, float(N), ALU.mult, ALU.add).then_inc(s["v_n0"], 1)
            dve.wait_ge(s["v_n0"], 1)
            v.tensor_scalar(exp_f[:], tile_f[:], n0[:, 0:1], None, ALU.is_ge).then_inc(s["v_exp"], 1)
            dve.wait_ge(s["v_exp"], 1)
            v.tensor_copy(exp_i[:], exp_f[:]).then_inc(s["v_expi"], 1)
            for c in range(HC):
                hidden_split(B - 1, c)
            shared_out(B - 1, 0)
            ffn_in_low(B, A)
            split_low("1", even_w, 2)
            shared_out(B - 1, 1)
            split_low("2", even_w, 2)
            shared_out(B - 1, 2)
            shared_out(B - 1, 3)

            def routed_out(t, d):
                dve.wait_ge(s["t_down"], t * 4 + (4 * B + d + 1))
                v.tensor_tensor(rg[:, d, :], routed_down[d][:, 0:C], rg[:, d, :], ALU.add).then_inc(s["v_y"], 1)

            def routed(t, at, last):
                for c in range(HC):
                    hidden_split(t + B, c)
                if not last:
                    ffn_in_low(t + (B + 1), A)
                dve.wait_ge(s["p_rgc"], t + 3)
                routed_out(t, 0)
                if not last:
                    split_low("1", other(at), t + 3)
                routed_out(t, 1)
                if not last:
                    split_low("2", other(at), t + 3)
                routed_out(t, 2)
                routed_out(t, 3)

            with dve.Fori(0, ROUTED // 2) as u:
                routed(u * 2, even_w, False)
                routed(u * 2 + 1, odd_w, False)
            routed(ROUTED - 1, even_w, True)

        @block.tensor
        def _(pe):
            T = nc.tensor

            def transposed_queries(b):
                pe.wait_ge(s["v_xh"], b + 1)
                for k in range(KC):
                    for i in range(TB):
                        last = T.transpose(Sb[:, k, P * i:P * i + P], xh[:, i, P * k:P * k + P], ident[:])
                    last.then_inc(s["t_T1"], 1)

            def project_q(b):
                for m in range(KC):
                    pe.wait_ge(s["a_xT"], b * 2 + 2)
                    for k in range(KC):
                        last = T.matmul(A[m], wq[:, k, P * m:P * m + P], xT[:, k, :], start=(k == 0), stop=(k == KC - 1))
                    last.then_inc(s["t_q"], 1)

            def scores(b, i, first):
                if i == 0:
                    pe.wait_ge(s["a_qT"], b * 2 + 2)
                    pe.wait_ge(s["p_kb"], b * 2 + 2)
                    if not first:
                        pe.wait_ge(s["v_min"], b * 4)
                else:
                    pe.wait_ge(s["v_min"], b * 4 + i)
                for k in range(KC):
                    for st in range(2):
                        q = slice(64 * st, 64 * st + 64)
                        last = T.matmul(Sb[:, st, C * k:C * k + C], qT[q, k, P * i:P * i + P],
                                        kblk[q, k, :, :].rearrange("p j n -> p (j n)"), start=True, stop=True)
                last.then_inc(s["t_s"], 1)

            def probs_T(b, i, first):
                pe.wait_ge(s["a_exp"], b * 4 + i + 1)
                if i > 0:
                    pe.wait_ge(s["a_PT"], b * 8 + 2 * i)
                for hlf in range(2):
                    for j in range(4):
                        q = 4 * hlf + j
                        last = T.transpose(A[hlf][:, P * j:P * j + P], SC[:, i % 2, P * q:P * q + P], ident[:])
                    last.then_inc(s["t_PT"], 1)

            def values(b, i, first):
                pe.wait_ge(s["a_PT"], b * 8 + 2 * i + 2)
                if i >= 2:
                    pe.wait_ge(s["v_zn"], b * 4 + i - 1)
                elif not first:
                    pe.wait_ge(s["v_x2l"], b * 2)
                if i == 1 and not first:
                    pe.wait_ge(s["v_slot"], b)
                for st in range(2):
                    for k in range(KC):
                        for jj in range(2):
                            q = (st * 2 + k) * 2 + jj
                            r = 4 * k + 2 * st + jj
                            last = T.matmul(Zb[i % 2][:, ZW * r:ZW * r + ZW], PT[:, q, :], vcur[:, ZW * r:ZW * r + ZW],
                                            start=True, stop=True)
                last.then_inc(s["t_z"], 1)

            def z_T(b):
                pe.wait_ge(s["v_zn"], b * 4 + 4)
                pe.wait_ge(s["a_PT"], b * 8 + 8)
                for k in range(KC):
                    for i in range(TB):
                        last = T.transpose(A[k][:, P * i:P * i + P], Zn[:, i, P * k:P * k + P], ident[:])
                    last.then_inc(s["t_ZT"], 1)

            def project_out(b):
                pe.wait_ge(s["a_ZT"], b * 2 + 2)
                for h in range(2):
                    for j in range(2):
                        i = 2 * h + j
                        for k in range(KC):
                            last = T.matmul(A[h][:, C * j:C * j + C], ZT[:, k, P * i:P * i + P], wo[:, k, :],
                                            start=(k == 0), stop=(k == KC - 1))
                    last.then_inc(s["t_wo"], 1)

            def rank(f):
                pe.wait_ge(s["v_sel"], f + 1)
                pe.wait_ge(s["v_x2l"], f * 2 + 2)
                o = Zb[1]
                T.matmul(o[:, 0:TB + 1], tri[:], sel[:], start=True, stop=False)
                T.matmul(o[:, 0:TB + 1], ones[:], R[:], start=False, stop=False)
                for j in range(1, TB + 1):
                    last = T.matmul(o[:, j:TB + 1], ones[:], sel[:, 0:TB + 1 - j], start=False, stop=(j == TB))
                last.then_inc(s["t_rank"], 1)

            def ffn_in_T(src, banks):
                for k in range(KC):
                    for i in range(TB):
                        last = T.transpose(banks[k][:, P * i:P * i + P], src[:, i, P * k:P * k + P], ident[:])
                    last.then_inc(s["t_T2"], 1)

            def shared_in_T(f):
                pe.wait_ge(s["v_row"], f * 4 + 4)
                pe.wait_ge(s["v_zn"], f * 4 + 4)
                ffn_in_T(row, Zb)

            def up(f, c, at=odd_w, routed=False):
                if c == 0:
                    pe.wait_ge(s["v_x2l"], f * 2 + 2)
                if routed:
                    pe.wait_ge(s["a_hf"], f * 8 + (c - 3))
                    if c in (2, 3):
                        pe.wait_ge(s["v_y"], f * 4 + (c - 3))
                elif c >= 2:
                    pe.wait_ge(s["a_hf"], f * 8 + c - 1)
                n = 0
                for k in range(KC):
                    for kind, xx in (("1h", x2h), ("1h", x2l), ("1l", x2h)):
                        last = T.matmul(ps[:, up_bank(c, routed), :], at[kind][:, k, P * c:P * c + P], xx[:, k, :],
                                        start=(n == 0), stop=(n == 3 * KC - 1))
                        n += 1
                last.then_inc(s["t_up"], 1)

            def down(f, d, at=odd_w, banks=U):
                if d == 0:
                    pe.wait_ge(s["v_hl"], f * 8 + 7)
                if len(banks) == 4:
                    if d < 2:
                        pe.wait_ge(s["v_y"], f * 4 + (d - 3))
                    else:
                        pe.wait_ge(s["a_hf"], f * 8 + 5 + d)
                elif d >= 2:
                    pe.wait_ge(s["v_y"], f * 4 + (d - 1))
                else:
                    pe.wait_ge(s["a_hf"], f * 8 + 7 + d)
                n = 0
                for c in range(HC):
                    if d == 0 and c == HC - 1:
                        pe.wait_ge(s["v_hl"], f * 8 + 8)
                    for hid, kind in ((hh, "2h"), (hh, "2l"), (hl, "2h")):
                        last = T.matmul(banks[d % len(banks)][:, 0:C], hid[:, c, P * d:P * d + P], at[kind][:, c, :],
                                        start=(n == 0), stop=(n == 3 * HC - 1))
                        n += 1
                last.then_inc(s["t_down"], 1)

            def with_relu_b1(e, half):
                if e == 0 and half == 0:
                    pe.wait_ge(s["d_w2e"], 16)
                    pe.wait_ge(s["a_rbc"], 2)
                    pe.wait_ge(s["v_vb"], 16)
                for c in range(half * HC // 2, half * HC // 2 + HC // 2):
                    last = T.matmul(U[e][:, 0:C], rbc[e][:, c, :], w2e[:, e, c, :], start=(c == 0), stop=(c == HC - 1))
                if half == 1:
                    last.then_inc(s["t_const"], 1)

            def attention(b, first, last):
                f = b - 1
                if not first:
                    pe.wait_ge(s["v_x1"], b * 2)
                project_q(b)
                if not first:
                    shared_in_T(f)
                scores(b, 0, first)
                if not first:
                    up(f, 0)
                    up(f, 1)
                scores(b, 1, first)
                if first:
                    with_relu_b1(0, 0)
                else:
                    up(f, 2)
                probs_T(b, 0, first)
                scores(b, 2, first)
                if first:
                    with_relu_b1(0, 1)
                else:
                    up(f, 3)
                values(b, 0, first)
                if not first:
                    up(f, 4)
                    rank(f)
                probs_T(b, 1, first)
                scores(b, 3, first)
                if first:
                    with_relu_b1(1, 0)
                else:
                    up(f, 5)
                values(b, 1, first)
                probs_T(b, 2, first)
                if first:
                    with_relu_b1(1, 1)
                else:
                    up(f, 6)
                    up(f, 7)
                values(b, 2, first)
                probs_T(b, 3, first)
                if not first:
                    down(f, 0)
                values(b, 3, first)
                if not first:
                    down(f, 1)
                z_T(b)
                if not first:
                    down(f, 2)
                if first:
                    pe.wait_ge(s["d_wo"], 16)
                project_out(b)
                if not last:
                    pe.wait_ge(s["v_min"], b * 4 + 4)
                    transposed_queries(b + 1)
                if not first:
                    down(f, 3)

            pe.wait_ge(s["p_ident"], 4)
            pe.wait_ge(s["d_ctx"], 16)
            for k in range(KC):
                for j in range(TB):
                    last = T.transpose(A[k][:, P * j:P * j + P], ctx_nat[:, j, P * k:P * k + P], ident[:])
                last.then_inc(s["t_ctx"], 1)
            pe.wait_ge(s["d_wk"], 16)
            for m in range(KC):
                pe.wait_ge(s["v_ctxT"], 2)
                for k in range(KC):
                    last = T.matmul(Zb[m].rearrange("p (b n) -> p b n", n=KEYS), wk[:, k, P * m:P * m + P], ctxT2[:, k, :, 0, :],
                                    start=(k == 0), stop=(k == KC - 1))
                last.then_inc(s["t_k"], 1)
            transposed_queries(0)
            pe.wait_ge(s["d_wv"], 16)
            vbank = A + U
            for b in range(B):
                for k in range(KC):
                    last = T.matmul(vbank[b // 2][:, (b % 2) * C:(b % 2) * C + C], ctxT2[:, k, b, :, :].rearrange("p d n -> p (d n)"),
                                    wv[:, k, :], start=(k == 0), stop=(k == KC - 1))
                if b % 2 == 1:
                    last.then_inc(s["t_v"], 1)
            pe.wait_ge(s["d_wq"], 16)
            pe.wait_ge(s["v_vb"], B)
            attention(0, True, False)
            pe.wait_ge(s["v_w1l"], 1)
            pe.wait_ge(s["v_w2l"], 1)
            pe.wait_ge(s["v_crow"], 2)
            with pe.Fori(1, B - 1) as b:
                attention(b, False, False)
            attention(B - 1, False, True)
            f = B - 1
            shared_in_T(f)
            rank(f)
            for c in range(HC):
                up(f, c)
            pe.wait_ge(s["d_xg"], 16)
            pe.wait_ge(s["v_x2l"], f * 2 + 2)
            ffn_in_T(xg, A)
            for d in range(TB):
                down(f, d)

            def routed(t, at, last):
                f = t + B
                pe.wait_ge(s["v_w1l"], t + 2)
                for c in range(HC):
                    up(f, c, at, True)
                if not last:
                    pe.wait_ge(s["d_xg"], t * 16 + 32)
                    pe.wait_ge(s["v_x2l"], f * 2 + 2)
                    ffn_in_T(xg, A)
                pe.wait_ge(s["v_w2l"], t + 2)
                for d in range(TB):
                    down(f, d, at, routed_down)

            with pe.Fori(0, ROUTED // 2) as u:
                routed(u * 2, even_w, False)
                routed(u * 2 + 1, odd_w, False)
            routed(ROUTED - 1, even_w, True)


_INS = ["x", "ctx_1024", "mask_Bx1xSxS2_ik1",
        "L0_xattn_WQ", "L0_xattn_bQ", "L0_xattn_WK", "L0_xattn_bK", "L0_xattn_WV", "L0_xattn_bV", "L0_xattn_WO", "L0_xattn_bO",
        "L0_ffn_gate_w", "L0_ffn_w1", "L0_ffn_b1", "L0_ffn_w2", "L0_ffn_b2", "L0_ffn_sw1", "L0_ffn_sb1", "L0_ffn_sw2", "L0_ffn_sb2"]
_OUTS = [((8, 512, 256), "float32")]


def _laid_out(name, a):
    short = name.split("_", 2)[-1]
    if short in ("WQ", "WK", "WV", "WO", "sw1", "sw2"):
        return a.reshape(-1, P, a.shape[1]).transpose(1, 0, 2)
    if short in ("w1", "w2"):
        return a.reshape(a.shape[0], -1, P, a.shape[2]).transpose(0, 2, 1, 3)
    if short in ("bQ", "bK", "sb1"):
        return a.reshape(-1, P).T
    if short == "b1":
        return a.reshape(a.shape[0], -1, P).transpose(2, 0, 1)
    return a


def kernel(**inputs):
    import numpy as _np
    import concourse.bacc as _bacc
    from concourse import mybir as _mybir
    from concourse.bass_utils import run_bass_kernel_spmd as _run

    nc = _bacc.Bacc("TRN2", target_bir_lowering=False, num_devices=1)
    arrays, args = {}, []
    for name in _INS:
        a = _np.ascontiguousarray(_laid_out(name, _np.asarray(inputs[name])))
        arrays[f"in_{name}_dram"] = a
        args.append(nc.dram_tensor(f"in_{name}_dram", a.shape, _mybir.dt.from_np(a.dtype), kind="ExternalInput").ap())
    for i, (shape, dtype) in enumerate(_OUTS):
        dt = _mybir.dt.from_np(_np.dtype(dtype))
        args.append(nc.dram_tensor(f"out_{i}_dram", shape, dt, kind="ExternalOutput").ap())
    attention_and_routed_ffn(nc, *args)
    r = _run(nc, [arrays], core_ids=[0])
    got = tuple(r.results[0][f"out_{i}_dram"] for i in range(len(_OUTS)))
    return got[0]
```

```python
import concourse.bass as bass
from concourse import mybir
from contextlib import ExitStack

F32 = mybir.dt.float32
F32R = mybir.dt.float32r
BF16 = mybir.dt.bfloat16
I32 = mybir.dt.int32
ALU = mybir.AluOpType
ACT = mybir.ActivationFunctionType
AX = mybir.AxisListType

P = 128


def attention_and_routed_ffn(nc, x, ctx, mask, WQ, bQ, WK, bK, WV, bV, WO, bO,
                             gate_w, w1, b1, w2, b2, sw1, sb1, sw2, sb2, out):
    B, S, C = x.shape
    KEYS = ctx.shape[1]
    H, D = 16, 16
    E, HID = w1.shape[0], w1.shape[3]
    KC = C // P
    TB = S // P
    NT = B * TB
    HC = HID // P
    N = B * S
    HALF = S // 2
    SLOTS = N + HALF
    ROUTED = N // S + 1
    ROW = C + 1
    PAIRS = H // 2
    ZW = 2 * (D + 1)
    NOBODY = 1 << 20
    MASKED = -1e9
    EPS = 1e-5
    NEWTON = 3
    RSTEPS = 2 + 3 * NEWTON

    xf = x.rearrange("b (p t) c -> p b (t c)", t=TB)
    outf = out.rearrange("b s c -> (b s) c")
    maskf = mask.rearrange("b a (p t) k -> p (b a) (t k)", t=TB)
    sorted_rows = nc.dram_tensor("sorted_rows", (SLOTS + HALF, ROW), F32).ap()
    resid = nc.dram_tensor("resid", (N, C), F32).ap()
    resid_v = resid.rearrange("(b p t) c -> p b (t c)", p=P, t=TB)
    sorted_v = sorted_rows.rearrange("(f j p) c -> p f j c", p=P, j=TB // 2)

    es = ExitStack()
    with es:
        def sb(name, shape, dt=F32):
            return es.enter_context(nc.sbuf_tensor(name, shape, dt))

        def sem(name):
            return es.enter_context(nc.semaphore(name))

        with ExitStack() as first_life:
            cap = first_life.enter_context(nc.sbuf_tensor("cap", [P, NT, KEYS], F32))
            X = first_life.enter_context(nc.sbuf_tensor("X", [P, NT, C], F32))
        even_w = {}
        for kind in ("2l", "1h", "1l", "2h"):
            even_w[kind] = sb("even_w" + kind, [P, KC, HID] if kind[0] == "1" else [P, HC, C], F32R)
        sb("rest_of_X", [P, NT // 4, C])
        odd_w = {}
        for kind in ("2l", "1h", "1l", "2h"):
            odd_w[kind] = sb("odd_w" + kind, [P, KC, HID] if kind[0] == "1" else [P, HC, C], F32R)
        wq = sb("wq", [P, KC, C])
        wo = sb("wo", [P, KC, C])
        kT = sb("kT", [P, KC, B * KEYS])
        kblk = sb("kblk", [P, KC, 4, KEYS])
        vblk = sb("vblk", [P, B, PAIRS * ZW])
        vcur = sb("vcur", [P, PAIRS * ZW])
        xh = sb("xh", [P, TB, C])
        with ExitStack() as first_life:
            xT = first_life.enter_context(nc.sbuf_tensor("xT", [P, KC, S], F32))
            qT = first_life.enter_context(nc.sbuf_tensor("qT", [P, KC, S], F32))
        xTh = sb("xTh", [P, KC, S], F32R)
        qTh = sb("qTh", [P, KC, S], F32R)
        SC = sb("SC", [P, 2, H * KEYS])
        PT = sb("PT", [P, PAIRS, P])
        Zn = sb("Zn", [P, TB, C])
        row = sb("row", [P, TB, ROW])
        with ExitStack() as middle_life:
            xTl, qTl, ZTh, ZTl = [middle_life.enter_context(nc.sbuf_tensor(n, [P, KC, S], F32R)) for n in ("xTl", "qTl", "ZTh", "ZTl")]
        stage1 = sb("stage1", [P, KC, HID])
        stage2 = sb("stage2", [P, HC, C])
        with ExitStack() as first_life:
            ZT = first_life.enter_context(nc.sbuf_tensor("ZT", [P, KC, S], F32))
        x2h = sb("x2h", [P, KC, S], F32R)
        x2l = sb("x2l", [P, KC, S], F32R)
        hf = sb("hf", [P, 2, S])
        hh = sb("hh", [P, HC, S], F32R)
        hl = sb("hl", [P, HC, S], F32R)
        with ExitStack() as middle_life:
            wqh, wql, woh, wol = [middle_life.enter_context(nc.sbuf_tensor(n, [P, KC, C], F32R)) for n in ("wqh", "wql", "woh", "wol")]
            kbh, kbl = [middle_life.enter_context(nc.sbuf_tensor(n, [P, KC, 4, KEYS], F32R)) for n in ("kbh", "kbl")]
        shared_region = sb("shared_region", [P, 2 * 4 * P * KC + TB * C])
        ctx_nat = shared_region[:, 0:TB * C].rearrange("p (j c) -> p j c", c=C)
        ctxT2 = shared_region[:, TB * C:TB * C + KC * B * 2 * KEYS].rearrange(
            "p (k b d n) -> p k b d n", k=KC, b=B, d=2)
        wk = stage1[:, 0, 0:KC * C].rearrange("p (k c) -> p k c", k=KC)
        wv = stage1[:, 1, 0:KC * C].rearrange("p (k c) -> p k c", k=KC)
        rg = [shared_region[:, 0:TB * C].rearrange("p (j c) -> p j c", c=C), Zn]
        xg = shared_region[:, TB * C:TB * C + TB * ROW].rearrange("p (j c) -> p j c", c=ROW)
        bo_b = sb("bo_b", [P, C])
        bv_b = sb("bv_b", [P, C])
        gw_b = sb("gw_b", [P, E, C])
        crow = sb("crow", [P, E, C])
        crow_cur = sb("crow_cur", [P, C])
        bq_c = sb("bq_c", [P, KC])
        bk_c = sb("bk_c", [P, KC])
        b1_c = sb("b1_c", [P, E, HC])
        b1_cur = sb("b1_cur", [P, HC])
        rb1 = sb("rb1", [P, E, HC])
        ident = sb("ident", [P, P])
        tri = sb("tri", [P, P], BF16)
        ones = sb("ones", [P, P], BF16)
        dmask = sb("dmask", [P, 4])
        tok_i = sb("tok_i", [P, NT], I32)
        ord_i = sb("ord_i", [P, NT], I32)
        tok_f = sb("tok_f", [P, NT])
        tok_r = sb("tok_r", [P, NT])
        tile_i = sb("tile_i", [P, ROUTED], I32)
        tile_f = sb("tile_f", [P, ROUTED])
        exp_f = sb("exp_f", [P, ROUTED])
        exp_i = sb("exp_i", [P, ROUTED], I32)
        start_i = tile_i
        start_f = sb("start_f", [P, ROUTED])
        ones_tiles, pair_end = sb("ones_tiles", [P, 1]), sb("pair_end", [P, 1])
        n0 = sb("n0", [P, 1])
        fill = sb("fill", [P, ROW])
        stA, stB = sb("stA", [P, TB, 6]), sb("stB", [P, TB, 6])
        mvA, mvB = sb("mvA", [P, TB, 2]), sb("mvB", [P, TB, 2])
        rsA, rsB = sb("rsA", [P, TB]), sb("rsB", [P, TB])
        rv, rt = sb("rv", [P, TB]), sb("rt", [P, TB])
        mx = sb("mx", [P, 2, H])
        rec = sb("rec", [P, 2, H])
        gsc = sb("gsc", [P, TB, E])
        sel = sb("sel", [P, TB + 1], BF16)
        R = sb("R", [P, TB + 1], BF16)
        rsum = sb("rsum", [P, 1])
        slotA, slotB = sb("slotA", [P, TB]), sb("slotB", [P, TB])
        slot_i = sb("slot_i", [P, TB], I32)
        ids = [sb("ids_even", [P, TB], I32), sb("ids_odd", [P, TB], I32)]

        ps = es.enter_context(nc.psum_tensor("ps", [P, 8, 512], F32))
        U = [ps[:, 0, :], ps[:, 1, :]]
        Sb = ps[:, 2:4, :]
        A = [ps[:, 4, :], ps[:, 5, :]]
        Zb = [ps[:, 6, :], ps[:, 7, :]]

        ranks = Zb[0][:, 0:TB + 1]

        names = """d_x d_ctx d_wk d_wv d_wq d_wo d_mask d_vec d_kvb d_w2e d_stage1 d_stage2 d_b1 d_fill d_res
            d_scat d_xg d_rg d_crow d_out
            p_ident p_dmask p_tabs p_fill p_vz p_kb p_xb p_sub p_rowid p_ids p_rgc p_sel0 p_wl
            v_ctxT v_kT v_vb v_tok v_tokr v_cvec v_cap v_rb1 v_crow v_st1 v_mv1 v_rs1 v_xh v_min v_max v_x2l v_hh v_hl
            v_rec v_zn v_y v_x1 v_st2 v_mv2 v_rs2 v_row v_gate v_sel v_sa v_sb v_slot v_rsum v_R v_exp
            v_expi v_w1l v_w2l
            a_ctxT a_rbc a_wqo v_wqo v_xTl v_qTl v_ZTl a_xT a_qT a_exp a_PT a_ZT a_x2h a_hf a_w1h a_w2h
            t_ctx t_k t_v t_const t_T1 t_q t_s t_PT t_z t_ZT t_wo t_rank t_T2 t_up t_down""".split()
        s = {n: sem(n) for n in names}

        routed_down = Zb + U

        def other(weights):
            return odd_w if weights is even_w else even_w

        def up_bank(c, routed):
            return (c + 2) % 4 if routed else c % 2

        def halves(bank):
            return bank.rearrange("p (j c) -> p j c", c=C)

        rbc = [hf[:, :, :].rearrange("p a n -> p (a n)").rearrange("p (c m) -> p c m", m=P),
               row[:, :, :].rearrange("p a n -> p (a n)")[:, 0:HC * P].rearrange("p (c m) -> p c m", m=P)]
        w2e = X[:, NT // 2:NT, :].rearrange("p (e j) c -> p e j c", e=E)

        block = es.enter_context(nc.Block())

        @block.sync
        def _(sp):
            sp.dma_start(ctx_nat, ctx.rearrange("b k c -> (b k) c").rearrange("(j p) c -> p j c", p=P)).then_inc(s["d_ctx"], 16)
            sp.dma_start(X[:, 0:TB, :].rearrange("p t c -> p (t c)"), xf[:, 0, :]).then_inc(s["d_x"], 16)
            sp.dma_start(wk, WK).then_inc(s["d_wk"], 16)
            sp.dma_start(wq[:], WQ).then_inc(s["d_wq"], 16)
            sp.dma_start(wv, WV).then_inc(s["d_wv"], 16)
            sp.dma_start(cap[:, :, :].bitcast(I32).rearrange("p (b t) k -> p b (t k)", t=TB), maskf).then_inc(s["d_mask"], 16)
            sp.dma_start(w2e, w2.rearrange("e p j c -> p e j c")).then_inc(s["d_w2e"], 16)
            sp.dma_start(wo[:], WO).then_inc(s["d_wo"], 16)
            sp.wait_ge(s["d_x"], 16)
            sp.dma_start(X[:, TB:2 * TB, :].rearrange("p t c -> p (t c)"), xf[:, 1, :]).then_inc(s["d_x"], 16)
            sp.wait_ge(s["t_v"], 4)
            sp.dma_start(stage1[:], sw1).then_inc(s["d_stage1"], 16)
            sp.dma_start(stage2[:], sw2).then_inc(s["d_stage2"], 16)
            for b in range(2, B // 2):
                sp.wait_ge(s["d_x"], 16 * b)
                sp.dma_start(X[:, TB * b:TB * b + TB, :].rearrange("p t c -> p (t c)"), xf[:, b, :]).then_inc(s["d_x"], 16)
            sp.wait_ge(s["p_fill"], 2)
            sp.dma_start(sorted_rows.rearrange("(p r) c -> p r c", p=P),
                         fill[:, :].unsqueeze(1).broadcast_to([P, (SLOTS + HALF) // P, ROW])).then_inc(s["d_fill"], 16)
            sp.wait_ge(s["t_const"], 2)
            for b in range(B // 2, B):
                sp.wait_ge(s["d_x"], 16 * b)
                sp.dma_start(X[:, TB * b:TB * b + TB, :].rearrange("p t c -> p (t c)"), xf[:, b, :]).then_inc(s["d_x"], 16)
            def resid_out(b):
                sp.wait_ge(s["v_y"], b * 4 + 4)
                sp.dma_start(resid_v[:, bass.ds(b, 1), :].rearrange("p b n -> p (b n)"),
                             X[:, bass.ds(b * TB, TB), :].rearrange("p t c -> p (t c)")).then_inc(s["d_res"], 16)

            def routed_in(t, first):
                e = sp.value_load(exp_i[0:1, bass.ds(t, 1)], min_val=0, max_val=E - 1)
                start = sp.value_load(start_i[0:1, bass.ds(t, 1)], min_val=0, max_val=SLOTS // HALF - 1)
                if not first:
                    sp.wait_ge(s["v_w1l"], t)
                sp.dma_start(stage1[:], w1[bass.ds(e, 1), :, :, :].rearrange("e p k n -> (e p) k n")).then_inc(s["d_stage1"], 16)
                if first:
                    sp.wait_ge(s["d_scat"], 64 * B)
                else:
                    sp.wait_ge(s["p_ids"], t)
                    sp.wait_ge(s["t_T2"], t * 2 + 2 * B)
                sp.dma_start(xg.rearrange("p (f j) c -> p f j c", f=2), sorted_v[:, bass.ds(start, 2), :, :]).then_inc(s["d_xg"], 16)
                if not first:
                    sp.wait_ge(s["v_w2l"], t)
                sp.dma_start(stage2[:], w2[bass.ds(e, 1), :, :, :].rearrange("e p j c -> (e p) j c")).then_inc(s["d_stage2"], 16)
                sp.wait_ge(s["p_rgc"], t + 2)
                sp.dma_start(crow_cur[:], crow[:, bass.ds(e, 1), :].rearrange("p e c -> p (e c)")).then_inc(s["d_crow"], 16)
                sp.wait_ge(s["a_hf"], t * 8 + 8 * B)
                sp.dma_start(b1_cur[:], b1_c[:, bass.ds(e, 1), :].rearrange("p e j -> p (e j)")).then_inc(s["d_b1"], 16)

            with sp.Fori(0, B - 1) as b:
                resid_out(b)
            sp.wait_ge(s["v_expi"], 2)
            routed_in(0, True)
            resid_out(B - 1)
            with sp.Fori(1, ROUTED) as t:
                routed_in(t, False)
            sp.wait_ge(s["d_res"], 16 * B)
            sp.wait_ge(s["d_out"], 64 * ROUTED - 32)

        @block.gpsimd
        def _(pool):
            g = nc.gpsimd
            g.memset(ones[:], 1.0).then_inc(s["p_ident"], 1)
            g.memset(dmask[:], 1.0).then_inc(s["p_ident"], 1)
            pool.wait_ge(s["p_ident"], 2)
            g.affine_select(out=ident[:], in_=ones[:], compare_op=ALU.is_equal, fill=0.0, base=0,
                            pattern=[[-1, P]], channel_multiplier=1).then_inc(s["p_ident"], 1)
            g.affine_select(out=tri[:], in_=ones[:], compare_op=ALU.is_gt, fill=0.0, base=0,
                            pattern=[[1, P]], channel_multiplier=-1).then_inc(s["p_ident"], 1)
            pool.wait_ge(s["p_ident"], 4)
            for r in range(2):
                g.affine_select(out=dmask[64 * r:64 * r + 64, :], in_=dmask[64 * r:64 * r + 64, :], compare_op=ALU.is_ge,
                                fill=0.0, base=0, pattern=[[-D, 4]], channel_multiplier=1).then_inc(s["p_dmask"], 1)
            pool.wait_ge(s["p_dmask"], 2)
            for r in range(2):
                g.affine_select(out=dmask[64 * r:64 * r + 64, :], in_=dmask[64 * r:64 * r + 64, :], compare_op=ALU.is_ge,
                                fill=0.0, base=D - 1, pattern=[[D, 4]], channel_multiplier=-1).then_inc(s["p_dmask"], 1)
            pool.wait_ge(s["p_dmask"], 4)
            g.memset(vblk[:], 0.0).then_inc(s["p_vz"], 1)
            pool.wait_ge(s["p_vz"], 1)
            vv = vblk[:, :, :].rearrange("p b (r w) -> p b r w", w=ZW)
            g.memset(vv[0:KEYS, :, :, D:D + 1], 1.0).then_inc(s["p_vz"], 1)
            g.memset(vv[KEYS:P, :, :, ZW - 1:ZW], 1.0).then_inc(s["p_vz"], 1)
            pool.wait_ge(s["p_vz"], 3)
            g.iota(tok_i[:], pattern=[[S, B], [1, TB]], base=0, channel_multiplier=TB).then_inc(s["p_tabs"], 1)
            g.iota(ord_i[:], pattern=[[P, NT]], base=0, channel_multiplier=1).then_inc(s["p_tabs"], 1)
            g.iota(tile_i[:], pattern=[[S, ROUTED]], base=0, channel_multiplier=0).then_inc(s["p_tabs"], 1)
            g.memset(sel[:], 0.0).then_inc(s["p_sel0"], 1)
            g.memset(R[:], 0.0).then_inc(s["p_sel0"], 1)
            g.memset(fill[:, 0:C], 0.0).then_inc(s["p_fill"], 1)
            g.memset(fill[:, C:ROW].bitcast(I32), NOBODY).then_inc(s["p_fill"], 1)

            def residual_bias(b):
                pool.wait_ge(s["d_x"], b * 16 + 16)
                pool.wait_ge(s["d_vec"], 5 * 16)
                pool.wait_ge(s["v_xh"], b + 1)
                g.tensor_tensor(X[:, bass.ds(b * TB, TB), :], X[:, bass.ds(b * TB, TB), :],
                                bo_b[:, :].unsqueeze(1).broadcast_to([P, TB, C]), ALU.add).then_inc(s["p_xb"], 1)

            def keys_build(b, first):
                if not first:
                    pool.wait_ge(s["t_s"], b * 4)
                    pool.wait_ge(s["t_z"], b * 4)
                g.tensor_tensor(kblk[:], kT[:, :, bass.ds(b * KEYS, KEYS)].unsqueeze(2).broadcast_to([P, KC, 4, KEYS]),
                                dmask[:, :].unsqueeze(1).unsqueeze(3).broadcast_to([P, KC, 4, KEYS]),
                                ALU.mult).then_inc(s["p_kb"], 1)
                if not first:
                    pool.compute_val(b * 4 - 1)
                    pool.wait_ge(s["p_kb"], 1)
                    pool.wait_ge(s["p_kb"], b * 4 - 1)
                    g.tensor_copy(kbh[:], kblk[:]).then_inc(s["p_kb"], 1)
                    pool.wait_ge(s["p_kb"], b * 4)
                    g.tensor_tensor(kbl[:], kblk[:], kbh[:, :, :, :].bitcast(F32), ALU.subtract).then_inc(s["p_kb"], 1)
                    values_of(b)

            def values_of(b):
                g.tensor_copy(vcur[:], vblk[:, bass.ds(b, 1), :].rearrange("p b w -> p (b w)")).then_inc(s["p_kb"], 1)

            def subtract_max(b, i):
                pool.wait_ge(s["v_max"], b * 4 + i + 1)
                sc = SC[:, i % 2, :].rearrange("p (h k) -> p h k", k=KEYS)
                g.tensor_tensor(sc, sc, mx[:, i % 2, :].unsqueeze(2).broadcast_to([P, H, KEYS]),
                                ALU.subtract).then_inc(s["p_sub"], 1)

            def scatter(f):
                pool.wait_ge(s["v_row"], f * 4 + 4)
                g.tensor_copy(row[:, :, C].bitcast(I32), tok_i[:, bass.ds(f * TB, TB)]).then_inc(s["p_rowid"], 1)
                pool.wait_ge(s["d_fill"], 16)
                pool.wait_ge(s["p_rowid"], f + 1)
                pool.wait_ge(s["v_slot"], f + 1)
                for j in range(TB):
                    g.indirect_dma_start(out=sorted_rows, out_offset=bass.IndirectOffsetOnAxis(ap=slot_i[:, j:j + 1], axis=0),
                                         in_=row[:, j, :], in_offset=None).then_inc(s["d_scat"], 16)

            def shared_low(kind, stage):
                pool.wait_ge(s[f"a_w{kind}h"], 1)
                g.tensor_tensor(odd_w[kind + "l"][:], stage[:], odd_w[kind + "h"][:, :, :].bitcast(F32), ALU.subtract).then_inc(s["p_wl"], 1)

            def attention(b, first):
                if not first:
                    residual_bias(b)
                else:
                    keys_build(0, True)
                    residual_bias(0)
                subtract_max(b, 0)
                subtract_max(b, 1)
                if first:
                    pool.wait_ge(s["v_vb"], 2 * B)
                    values_of(0)
                subtract_max(b, 2)
                subtract_max(b, 3)
                if first:
                    shared_low("1", stage1)
                else:
                    scatter(b - 1)

            pool.wait_ge(s["v_kT"], 2)
            pool.wait_ge(s["p_dmask"], 4)
            attention(0, True)
            keys_build(1, False)
            shared_low("2", stage2)
            with pool.Fori(1, B - 1) as b:
                attention(b, False)
                keys_build(b + 1, False)
            attention(B - 1, False)
            scatter(B - 1)
            pool.wait_ge(s["t_ctx"], 2)
            pool.wait_ge(s["t_v"], 4)
            g.memset(rg[0], 0.0).then_inc(s["p_rgc"], 1)
            g.memset(rg[1][:], 0.0).then_inc(s["p_rgc"], 1)

            def gather(t, odd):
                pool.compute_val(t * 16 + 16)
                pool.wait_ge(s["d_xg"], 16)
                pool.wait_ge(s["d_xg"], t * 16 + 16)
                g.tensor_copy(ids[odd][:], xg[:, :, C].bitcast(I32)).then_inc(s["p_ids"], 1)
                pool.compute_val(t + 1)
                pool.wait_ge(s["d_res"], 16 * B)
                pool.wait_ge(s["p_rgc"], 2)
                pool.wait_ge(s["p_ids"], t + 1)
                for j in range(TB):
                    g.indirect_dma_start(out=rg[odd][:, j, :], out_offset=None, in_=resid,
                                         in_offset=bass.IndirectOffsetOnAxis(ap=ids[odd][:, j:j + 1], axis=0),
                                         bounds_check=N - 1, oob_is_err=False).then_inc(s["d_rg"], 16)
                pool.wait_ge(s["d_rg"], t * 64 + 64)
                pool.wait_ge(s["d_crow"], t * 16 + 16)
                r = rg[odd][:, :, :] if odd else rg[odd]
                g.tensor_tensor(r, r, crow_cur[:, :].unsqueeze(1).broadcast_to([P, TB, C]), ALU.add).then_inc(s["p_rgc"], 1)

            def routed_out(t, odd, last):
                for j in range(TB // 2 if last else TB):
                    pool.compute_val(t * 4 + (4 * B + j + 1))
                    pool.wait_ge(s["v_y"], 4 * B)
                    pool.wait_ge(s["v_y"], t * 4 + (4 * B + j + 1))
                    g.indirect_dma_start(out=outf, out_offset=bass.IndirectOffsetOnAxis(ap=ids[odd][:, j:j + 1], axis=0),
                                         in_=rg[odd][:, j, :], in_offset=None,
                                         bounds_check=N - 1, oob_is_err=False).then_inc(s["d_out"], 16)

            gather(0, 0)
            gather(1, 1)
            routed_out(0, 0, False)
            with pool.Fori(0, ROUTED // 2 - 1) as u:
                for odd in (1, 0):
                    t = u * 2 + (2 - odd)
                    pool.wait_ge(s["d_out"], t * 64)
                    gather(t + 1, 1 - odd)
                    routed_out(t, odd, False)
            pool.wait_ge(s["d_out"], (ROUTED - 2) * 64)
            gather(ROUTED - 1, 0)
            routed_out(ROUTED - 2, 1, False)
            routed_out(ROUTED - 1, 0, True)

        @block.scalar
        def _(act):
            a = nc.scalar
            act.dma_start(bk_c[:], bK).then_inc(s["d_kvb"], 16)
            act.dma_start(bv_b[:], bV.partition_broadcast(P)).then_inc(s["d_kvb"], 16)
            act.dma_start(bq_c[:], bQ).then_inc(s["d_kvb"], 16)
            act.dma_start(b1_c[:], b1).then_inc(s["d_vec"], 16)
            act.dma_start(bo_b[:], bO.partition_broadcast(P)).then_inc(s["d_vec"], 16)
            act.dma_start(gw_b[:], gate_w.partition_broadcast(P)).then_inc(s["d_vec"], 16)
            act.dma_start(crow[:], b2.partition_broadcast(P)).then_inc(s["d_vec"], 16)
            act.dma_start(crow_cur[:], sb2.partition_broadcast(P)).then_inc(s["d_vec"], 16)
            act.dma_start(b1_cur[:], sb1).then_inc(s["d_b1"], 16)

            def queries_T(b):
                for k in range(KC):
                    act.wait_ge(s["t_T1"], b * 2 + k + 1)
                    act.wait_ge(s["t_q"], b * 2)
                    a.activation(xTh[:, k, :], Sb[:, k, :], ACT.Copy).then_inc(s["a_xT"], 1)

            def project_q(b, q=qTh, banks=Zb):
                for m in range(KC):
                    act.wait_ge(s["t_q"], b * 2 + m + 1)
                    a.activation(q[:, m, :], banks[m], ACT.Identity, bias=bq_c[:, m:m + 1]).then_inc(s["a_qT"], 1)

            def expo(b, i):
                act.wait_ge(s["p_sub"], b * 4 + i + 1)
                a.activation(SC[:, i % 2, :], SC[:, i % 2, :], ACT.Exp).then_inc(s["a_exp"], 1)

            def probs_T(b, i):
                for hlf in range(2):
                    act.wait_ge(s["t_PT"], b * 8 + 2 * i + hlf + 1)
                    if i > 0 and hlf == 0:
                        act.wait_ge(s["t_z"], b * 4 + i)
                    a.activation(PT[:, 4 * hlf:4 * hlf + 4, :].rearrange("p a n -> p (a n)"), A[hlf], ACT.Copy).then_inc(s["a_PT"], 1)

            def z_T(b, z=ZTh):
                for k in range(KC):
                    act.wait_ge(s["t_ZT"], b * 2 + k + 1)
                    a.activation(z[:, k, :], A[k], ACT.Copy).then_inc(s["a_ZT"], 1)

            def ffn_in_high(f):
                for k in range(KC):
                    act.wait_ge(s["t_T2"], f * 2 + k + 1)
                    a.activation(x2h[:, k, :], A[k], ACT.Copy).then_inc(s["a_x2h"], 1)

            def split_high(kind, at):
                a.activation(at[kind + "h"][:], (stage1 if kind == "1" else stage2)[:], ACT.Copy).then_inc(s[f"a_w{kind}h"], 1)

            def hidden(f, c, routed=False, n=S):
                act.wait_ge(s["t_up"], f * 8 + c + 1)
                if c >= 2:
                    act.wait_ge(s["v_hl"], f * 8 + c - 1)
                a.activation(hf[:, c % 2, 0:n], ps[:, up_bank(c, routed), 0:n], ACT.Relu, bias=b1_cur[:, c:c + 1]).then_inc(s["a_hf"], 1)

            def attention(b, first, last):
                f = b - 1
                if first:
                    project_q(0, qT, A)
                    act.wait_ge(s["v_rb1"], 1)
                    for e in range(E):
                        a.activation(rbc[e], rb1[:, e, :].unsqueeze(2).broadcast_to([P, HC, P]), ACT.Copy).then_inc(s["a_rbc"], 1)
                else:
                    ffn_in_high(f)
                    hidden(f, 0)
                expo(b, 0)
                if not first:
                    hidden(f, 1)
                    hidden(f, 2)
                probs_T(b, 0)
                expo(b, 1)
                if not first:
                    hidden(f, 3)
                probs_T(b, 1)
                expo(b, 2)
                if not first:
                    hidden(f, 4)
                if first:
                    act.wait_ge(s["d_stage1"], 16)
                    split_high("1", odd_w)
                else:
                    hidden(f, 5)
                probs_T(b, 2)
                expo(b, 3)
                if not first:
                    hidden(f, 6)
                probs_T(b, 3)
                if first:
                    act.wait_ge(s["d_stage2"], 16)
                    split_high("2", odd_w)
                    a.activation(wqh[:], wq[:], ACT.Copy).then_inc(s["a_wqo"], 1)
                    act.wait_ge(s["d_wo"], 16)
                    a.activation(woh[:], wo[:], ACT.Copy).then_inc(s["a_wqo"], 1)
                    queries_T(1)
                    z_T(0, ZT)
                    project_q(1)
                else:
                    hidden(f, 7)
                    z_T(b)
                    if not last:
                        queries_T(b + 1)
                        project_q(b + 1)

            for k in range(KC):
                act.wait_ge(s["v_ctxT"], k + 1)
                a.activation(ctxT2[:, k, :, 1, :], A[k].rearrange("p (b n) -> p b n", n=KEYS), ACT.Copy).then_inc(s["a_ctxT"], 1)
            act.wait_ge(s["d_kvb"], 3 * 16)
            for k in range(KC):
                act.wait_ge(s["t_T1"], k + 1)
                a.activation(xT[:, k, :], Sb[:, k, :], ACT.Copy).then_inc(s["a_xT"], 1)
            attention(0, True, False)
            act.wait_ge(s["d_b1"], 16)
            with act.Fori(1, B - 1) as b:
                attention(b, False, False)
            attention(B - 1, False, True)
            ffn_in_high(B - 1)
            for c in range(HC):
                hidden(B - 1, c)

            def prepare(t, at, first=False):
                if not first:
                    ffn_in_high(t + B)
                act.wait_ge(s["d_stage1"], t * 16 + 32)
                split_high("1", at)
                if first:
                    ffn_in_high(t + B)
                act.wait_ge(s["d_stage2"], t * 16 + 32)
                split_high("2", at)

            def routed(t, at, last):
                act.wait_ge(s["d_b1"], t * 16 + 32)
                for c in range(HC):
                    hidden(t + B, c, True, HALF if last else S)
                if not last:
                    prepare(t + 1, other(at))

            act.wait_ge(s["d_res"], 16 * (B - 2))
            prepare(0, even_w, True)
            with act.Fori(0, ROUTED // 2) as u:
                routed(u * 2, even_w, False)
                routed(u * 2 + 1, odd_w, False)
            routed(ROUTED - 1, even_w, True)

        @block.vector
        def _(dve):
            v = nc.vector

            def inverse_root(b, mv, rs, done):
                v.tensor_scalar(rv[:], mv[:, :, 1], EPS, None, ALU.add).then_inc(done, 1)
                dve.wait_ge(done, b * RSTEPS + 1)
                v.tensor_scalar(rs[:, :].bitcast(I32), rv[:, :].bitcast(I32), -0.5, float(0x5F3759DF),
                                ALU.mult, ALU.add).then_inc(done, 1)
                dve.wait_ge(done, b * RSTEPS + 2)
                for k in range(NEWTON):
                    v.tensor_tensor(rt[:], rs[:], rs[:], ALU.mult).then_inc(done, 1)
                    dve.wait_ge(done, b * RSTEPS + 3 * k + 3)
                    v.scalar_tensor_tensor(out=rt[:], in0=rt[:], scalar=-0.5, in1=rv[:], op0=ALU.mult, op1=ALU.mult).then_inc(done, 1)
                    dve.wait_ge(done, b * RSTEPS + 3 * k + 4)
                    v.scalar_tensor_tensor(out=rs[:], in0=rt[:], scalar=1.5, in1=rs[:], op0=ALU.add, op1=ALU.mult).then_inc(done, 1)
                    dve.wait_ge(done, b * RSTEPS + 3 * k + 5)

            def norm1_stats(b):
                dve.wait_ge(s["d_x"], 16)
                dve.wait_ge(s["d_x"], b * 16 + 16)
                for i in range(TB):
                    last = v.bn_stats(stA[:, i, :], X[:, bass.ds(b * TB + i, 1), :].rearrange("p a c -> p (a c)"))
                last.then_inc(s["v_st1"], 1)
                dve.compute_val(b + 1)
                dve.wait_ge(s["v_st1"], 1)
                dve.wait_ge(s["v_st1"], b + 1)
                for i in range(TB):
                    last = v.bn_aggr(mvA[:, i, :], stA[:, i, :])
                last.then_inc(s["v_mv1"], 1)

            def norm1_root(b):
                dve.wait_ge(s["v_mv1"], b + 1)
                inverse_root(b, mvA, rsA, s["v_rs1"])

            def norm1(b):
                if not isinstance(b, int) or b > 0:
                    dve.wait_ge(s["t_T1"], b * 2)
                for i in range(TB):
                    last = v.tensor_scalar(xh[:, i, :], X[:, bass.ds(b * TB + i, 1), :].rearrange("p a c -> p (a c)"),
                                           mvA[:, i, 0:1], rsA[:, i:i + 1], ALU.subtract, ALU.mult)
                last.then_inc(s["v_xh"], 1)

            def queries_low(b):
                for k in range(KC):
                    dve.wait_ge(s["a_xT"], b * 2 + k + 1)
                    v.tensor_tensor(xTl[:, k, :], Sb[:, k, :], xTh[:, k, :].bitcast(F32), ALU.subtract).then_inc(s["v_xTl"], 1)

            def project_q_low(b):
                for m in range(KC):
                    dve.wait_ge(s["a_qT"], b * 2 + m + 1)
                    v.scalar_tensor_tensor(out=qTl[:, m, :], in0=Zb[m], scalar=bq_c[:, m:m + 1], in1=qTh[:, m, :].bitcast(F32),
                                           op0=ALU.add, op1=ALU.subtract).then_inc(s["v_qTl"], 1)

            def z_low(b):
                for k in range(KC):
                    dve.wait_ge(s["a_ZT"], b * 2 + k + 1)
                    v.tensor_tensor(ZTl[:, k, :], A[k], ZTh[:, k, :].bitcast(F32), ALU.subtract).then_inc(s["v_ZTl"], 1)

            def masked_max(b, i, first):
                dve.wait_ge(s["t_s"], b * 4 + i + 1)
                if i >= 2:
                    dve.wait_ge(s["t_PT"], b * 8 + 2 * i - 2)
                elif not first:
                    dve.wait_ge(s["t_PT"], b * 8 - 4 + 2 * i)
                sc = SC[:, i % 2, :].rearrange("p (h k) -> p h k", k=KEYS)
                v.tensor_tensor(sc, Sb.rearrange("p s (h k) -> p (s h) k", k=KEYS),
                                cap[:, bass.ds(b * TB + i, 1), :].broadcast_to([P, H, KEYS]), ALU.min).then_inc(s["v_min"], 1)
                dve.wait_ge(s["v_min"], b * 4 + i + 1)
                v.tensor_reduce(mx[:, i % 2, :], sc, AX.X, ALU.max).then_inc(s["v_max"], 1)

            def normalise(b, i):
                dve.wait_ge(s["t_z"], b * 4 + i + 1)
                z = Zb[i % 2][:, 0:H * (D + 1)].rearrange("p (h w) -> p h w", w=D + 1)
                v.reciprocal(rec[:, i % 2, :], z[:, :, D]).then_inc(s["v_rec"], 1)
                dve.wait_ge(s["v_rec"], b * 4 + i + 1)
                v.tensor_tensor(Zn[:, i, :].rearrange("p (h d) -> p h d", d=D), z[:, :, 0:D],
                                rec[:, i % 2, :].unsqueeze(2).broadcast_to([P, H, D]), ALU.mult).then_inc(s["v_zn"], 1)

            def attended(b):
                dve.wait_ge(s["p_xb"], b + 1)
                for h in range(2):
                    dve.wait_ge(s["t_wo"], b * 2 + h + 1)
                    xs = X[:, bass.ds(b * TB + 2 * h, 2), :]
                    v.tensor_tensor(xs, halves(A[h]), xs, ALU.add).then_inc(s["v_x1"], 1)

            def norm2_stats(b):
                dve.wait_ge(s["v_x1"], 2)
                dve.wait_ge(s["v_x1"], b * 2 + 2)
                for i in range(TB):
                    last = v.bn_stats(stB[:, i, :], X[:, bass.ds(b * TB + i, 1), :].rearrange("p a c -> p (a c)"))
                last.then_inc(s["v_st2"], 1)
                dve.compute_val(b + 1)
                dve.wait_ge(s["v_st2"], 1)
                dve.wait_ge(s["v_st2"], b + 1)
                for i in range(TB):
                    last = v.bn_aggr(mvB[:, i, :], stB[:, i, :])
                last.then_inc(s["v_mv2"], 1)

            def norm2(b, first):
                dve.wait_ge(s["v_mv2"], b + 1)
                inverse_root(b, mvB, rsB, s["v_rs2"])
                if not first:
                    dve.wait_ge(s["d_scat"], b * 64)
                    dve.wait_ge(s["t_T2"], b * 2)
                for i in range(TB):
                    v.tensor_scalar(row[:, i, 0:C], X[:, bass.ds(b * TB + i, 1), :].rearrange("p a c -> p (a c)"),
                                    mvB[:, i, 0:1], rsB[:, i:i + 1], ALU.subtract, ALU.mult).then_inc(s["v_row"], 1)

            def gate(b, e):
                dve.wait_ge(s["v_row"], b * 4 + 4)
                for i in range(TB):
                    if e > 0:
                        dve.wait_ge(s["v_gate"], b * 8 + i + 1)
                    v.tensor_tensor_reduce(out=Zn[:, i, :], in0=row[:, i, 0:C], in1=gw_b[:, e, :], scale=1.0, scalar=0.0,
                                           op0=ALU.mult, op1=ALU.add, accum_out=gsc[:, i, e:e + 1]).then_inc(s["v_gate"], 1)

            def choose(b):
                dve.wait_ge(s["v_gate"], b * 8 + 8)
                v.tensor_tensor(sel[:, 0:TB], gsc[:, :, 1], gsc[:, :, 0], ALU.is_gt).then_inc(s["v_sel"], 1)

            def slots(f):
                dve.wait_ge(s["t_rank"], f + 1)
                r = ranks[:, 0:TB]
                v.scalar_tensor_tensor(out=slotA[:], in0=r, scalar=-1.0, in1=tok_f[:, bass.ds(f * TB, TB)],
                                       op0=ALU.mult, op1=ALU.add).then_inc(s["v_sa"], 1)
                v.tensor_tensor(slotB[:], sel[:, 0:TB], tok_r[:, bass.ds(f * TB, TB)], ALU.mult).then_inc(s["v_sb"], 1)
                v.tensor_reduce(rsum[:], sel[:, 0:TB], AX.X, ALU.add).then_inc(s["v_rsum"], 1)
                dve.wait_ge(s["v_sa"], f + 1)
                dve.wait_ge(s["v_sb"], f + 1)
                v.tensor_tensor(slot_i[:], slotA[:], slotB[:], ALU.add).then_inc(s["v_slot"], 1)
                dve.wait_ge(s["v_rsum"], f + 1)
                v.tensor_tensor(R[:], R[:], rsum[:, :].broadcast_to([P, TB + 1]), ALU.add).then_inc(s["v_R"], 1)

            def ffn_in_low(f):
                for k in range(KC):
                    dve.wait_ge(s["a_x2h"], f * 2 + k + 1)
                    v.tensor_tensor(x2l[:, k, :], A[k], x2h[:, k, :].bitcast(F32), ALU.subtract).then_inc(s["v_x2l"], 1)

            def hidden_split(f, c, n=S):
                dve.wait_ge(s["a_hf"], f * 8 + c + 1)
                v.tensor_copy(hh[:, c, 0:n], hf[:, c % 2, 0:n]).then_inc(s["v_hh"], 1)
                dve.wait_ge(s["v_hh"], f * 8 + c + 1)
                v.tensor_tensor(hl[:, c, 0:n], hf[:, c % 2, 0:n], hh[:, c, 0:n].bitcast(F32), ALU.subtract).then_inc(s["v_hl"], 1)

            def shared_out(f, d):
                dve.wait_ge(s["t_down"], f * 4 + d + 1)
                xs = X[:, bass.ds(f * TB + d, 1), :].rearrange("p a c -> p (a c)")
                v.tensor_tensor(xs, U[d % 2][:, 0:C], xs, ALU.add).then_inc(s["v_y"], 1)

            def split_low(kind, at, splits):
                dve.wait_ge(s[f"a_w{kind}h"], splits)
                v.tensor_tensor(at[kind + "l"][:], (stage1 if kind == "1" else stage2)[:], at[kind + "h"][:, :, :].bitcast(F32),
                                ALU.subtract).then_inc(s[f"v_w{kind}l"], 1)

            def attention(b, first, last):
                f = b - 1
                if first:
                    masked_max(0, 0, True)
                    values_in(1)
                else:
                    ffn_in_low(f)
                masked_max(b, 1, first)
                if first:
                    values_in(2)
                    values_in(3)
                if not first:
                    hidden_split(f, 0)
                    hidden_split(f, 1)
                    gate(f, 0)
                masked_max(b, 2, first)
                if not first:
                    hidden_split(f, 2)
                    gate(f, 1)
                    choose(f)
                normalise(b, 0)
                if not first:
                    hidden_split(f, 3)
                masked_max(b, 3, first)
                if not first:
                    hidden_split(f, 4)
                    slots(f)
                    hidden_split(f, 5)
                normalise(b, 1)
                if not last:
                    norm1_stats(b + 1)
                if not first:
                    hidden_split(f, 6)
                    normalise(b, 2)
                if first:
                    norm1_root(1)
                    normalise(0, 2)
                    norm1(1)
                    normalise(0, 3)
                    dve.wait_ge(s["a_wqo"], 2)
                    v.tensor_tensor(wql[:], wq[:], wqh[:, :, :].bitcast(F32), ALU.subtract).then_inc(s["v_wqo"], 1)
                    v.tensor_tensor(wol[:], wo[:], woh[:, :, :].bitcast(F32), ALU.subtract).then_inc(s["v_wqo"], 1)
                    dve.wait_ge(s["p_wl"], 1)
                    queries_low(1)
                    for e in range(E):
                        dve.wait_ge(s["t_const"], e + 1)
                        v.tensor_tensor(crow[:, 1 - e, :], U[e][:, 0:C], crow_cur[:], ALU.add).then_inc(s["v_crow"], 1)
                    attended(0)
                    norm2_stats(0)
                    project_q_low(1)
                    norm2(0, True)
                    masked_max(1, 0, False)
                else:
                    hidden_split(f, 7)
                    normalise(b, 3)
                    if not last:
                        norm1_root(b + 1)
                        norm1(b + 1)
                    z_low(b)
                    if not last:
                        queries_low(b + 1)
                    shared_out(f, 0)
                    shared_out(f, 1)
                    attended(b)
                    norm2_stats(b)
                    if not last:
                        project_q_low(b + 1)
                    norm2(b, False)
                    shared_out(f, 2)
                    if not last:
                        masked_max(b + 1, 0, False)
                    shared_out(f, 3)

            for k in range(KC):
                dve.wait_ge(s["t_ctx"], k + 1)
                v.tensor_copy(ctxT2[:, k, :, 0, :], A[k].rearrange("p (b n) -> p b n", n=KEYS)).then_inc(s["v_ctxT"], 1)
            norm1_stats(0)
            norm1_root(0)
            norm1(0)
            dve.wait_ge(s["d_kvb"], 3 * 16)
            for m in range(KC):
                dve.wait_ge(s["t_k"], m + 1)
                v.tensor_scalar(kT[:, m, :], Zb[m], bk_c[:, m:m + 1], 0.25, ALU.add, ALU.mult).then_inc(s["v_kT"], 1)
            dve.wait_ge(s["d_mask"], 16)
            v.tensor_scalar(cap[:], cap[:, :, :].bitcast(I32), 0.0, -3e38, ALU.is_equal, ALU.mult).then_inc(s["v_cap"], 1)
            dve.wait_ge(s["v_cap"], 1)
            v.tensor_scalar(cap[:], cap[:], 1.5e38, MASKED, ALU.add, ALU.max).then_inc(s["v_cap"], 1)
            vb = vblk[:, :, :].rearrange("p b (r o w) -> p b r o w", o=2, w=D + 1)
            vbank = U + Zb

            def values_in(pair):
                for b in (2 * pair, 2 * pair + 1):
                    dve.wait_ge(s["t_v"], pair + 1)
                    src = vbank[pair][:, (b % 2) * C:(b % 2) * C + C].rearrange("p (r o d) -> p r o d", o=2, d=D)
                    bias = bv_b[:, :].rearrange("p (r o d) -> p r o d", o=2, d=D)
                    for o in range(2):
                        q = slice(64 * o, 64 * o + 64)
                        v.tensor_tensor(vb[q, b, :, o, 0:D], src[q, :, o, :], bias[q, :, o, :], ALU.add).then_inc(s["v_vb"], 1)

            dve.wait_ge(s["d_vec"], 5 * 16)
            v.tensor_scalar(rb1[:], b1_c[:], 0.0, None, ALU.max).then_inc(s["v_rb1"], 1)
            v.tensor_tensor(crow_cur[:], crow_cur[:], crow[:, 0, :], ALU.add).then_inc(s["v_cvec"], 1)
            dve.wait_ge(s["v_cvec"], 1)
            v.tensor_tensor(crow_cur[:], crow_cur[:], crow[:, 1, :], ALU.add).then_inc(s["v_cvec"], 1)
            dve.wait_ge(s["v_cvec"], 2)
            dve.wait_ge(s["p_vz"], 3)
            values_in(0)
            dve.wait_ge(s["p_tabs"], 3)
            v.tensor_copy(tok_f[:], ord_i[:]).then_inc(s["v_tok"], 1)
            v.tensor_copy(tile_f[:], tile_i[:])
            dve.wait_ge(s["v_tok"], 1)
            v.tensor_scalar(tok_r[:], tok_f[:], -1.0, float(SLOTS - 1), ALU.mult, ALU.add).then_inc(s["v_tokr"], 1)
            dve.wait_ge(s["v_tokr"], 1)
            dve.wait_ge(s["v_cap"], 2)
            dve.wait_ge(s["p_sel0"], 2)
            attention(0, True, False)
            with dve.Fori(1, B - 1) as b:
                attention(b, False, False)
            attention(B - 1, False, True)
            gate(B - 1, 0)
            ffn_in_low(B - 1)
            gate(B - 1, 1)
            choose(B - 1)
            hidden_split(B - 1, 0)
            hidden_split(B - 1, 1)
            slots(B - 1)
            hidden_split(B - 1, 2)
            def step(k):
                dve.wait_ge(s["v_exp"], k)

            FULL = ROUTED - 1
            v.tensor_scalar(n0[:], ranks[:, TB:TB + 1], -1.0, float(N), ALU.mult, ALU.add).then_inc(s["v_exp"], 1)
            step(1)
            v.tensor_scalar(pair_end[:], n0[:], -float(HALF), None, ALU.add).then_inc(s["v_exp"], 1)
            step(2)
            v.tensor_scalar(exp_f[:, 0:FULL], tile_f[:, 0:FULL], pair_end[:, 0:1], None, ALU.is_ge).then_inc(s["v_exp"], 1)
            step(3)
            v.tensor_reduce(ones_tiles[:], exp_f[:, 0:FULL], AX.X, ALU.add).then_inc(s["v_exp"], 1)
            v.scalar_tensor_tensor(out=start_f[:, 0:FULL], in0=tile_f[:, 0:FULL], scalar=1.0 / HALF, in1=exp_f[:, 0:FULL],
                                   op0=ALU.mult, op1=ALU.add).then_inc(s["v_exp"], 1)
            step(4)
            v.tensor_scalar(start_f[:, FULL:ROUTED], ones_tiles[:], -2.0, float(2 * FULL), ALU.mult, ALU.add).then_inc(s["v_exp"], 1)
            v.tensor_scalar(pair_end[:], ones_tiles[:], -float(S), float(N), ALU.mult, ALU.add).then_inc(s["v_exp"], 1)
            step(7)
            v.tensor_tensor(exp_f[:, FULL:ROUTED], pair_end[:], n0[:], ALU.is_ge).then_inc(s["v_exp"], 1)
            step(8)
            v.tensor_copy(exp_i[:], exp_f[:]).then_inc(s["v_expi"], 1)
            v.tensor_copy(start_i[:], start_f[:]).then_inc(s["v_expi"], 1)
            for c in range(3, HC):
                hidden_split(B - 1, c)
            shared_out(B - 1, 0)
            split_low("1", even_w, 2)
            shared_out(B - 1, 1)
            ffn_in_low(B)
            split_low("2", even_w, 2)
            shared_out(B - 1, 2)
            shared_out(B - 1, 3)

            def routed_out(t, odd, d):
                dve.wait_ge(s["t_down"], t * 4 + (4 * B + d + 1))
                v.tensor_tensor(rg[odd][:, d, :], routed_down[d][:, 0:C], rg[odd][:, d, :], ALU.add).then_inc(s["v_y"], 1)

            def routed(t, odd, last):
                for c in range(HC):
                    hidden_split(t + B, c, HALF if last else S)
                if not last:
                    ffn_in_low(t + (B + 1))
                dve.wait_ge(s["p_rgc"], t + 3)
                routed_out(t, odd, 0)
                if not last:
                    split_low("1", (odd_w, even_w)[odd], t + 3)
                routed_out(t, odd, 1)
                if not last:
                    split_low("2", (odd_w, even_w)[odd], t + 3)
                    routed_out(t, odd, 2)
                    routed_out(t, odd, 3)

            with dve.Fori(0, ROUTED // 2) as u:
                routed(u * 2, 0, False)
                routed(u * 2 + 1, 1, False)
            routed(ROUTED - 1, 0, True)

        @block.tensor
        def _(pe):
            T = nc.tensor

            def transposed_queries(b, first=False):
                pe.wait_ge(s["v_xh"], b + 1)
                if not first:
                    pe.wait_ge(s["v_min"], b * 4)
                for k in range(KC):
                    for i in range(TB):
                        last = T.transpose(Sb[:, k, P * i:P * i + P], xh[:, i, P * k:P * k + P], ident[:])
                    last.then_inc(s["t_T1"], 1)

            def project_q_whole():
                for m in range(KC):
                    pe.wait_ge(s["a_xT"], 2)
                    for k in range(KC):
                        last = T.matmul(A[m], wq[:, k, P * m:P * m + P], xT[:, k, :], start=(k == 0), stop=(k == KC - 1))
                    last.then_inc(s["t_q"], 1)

            def project_q(b):
                pe.wait_ge(s["v_zn"], b * 4)
                pe.wait_ge(s["a_xT"], b * 2 + 2)
                for m in range(KC):
                    n = 0
                    for w, xx in ((wqh, xTh), (wql, xTh), (wqh, xTl)):
                        if xx is xTl:
                            pe.wait_ge(s["v_xTl"], b * 2)
                        for k in range(KC):
                            last = T.matmul(Zb[m], w[:, k, P * m:P * m + P], xx[:, k, :], start=(n == 0), stop=(n == 3 * KC - 1))
                            n += 1
                    last.then_inc(s["t_q"], 1)

            def scores(b, i, first):
                if i == 0:
                    pe.wait_ge(s["a_qT"], b * 2 + 2)
                    pe.wait_ge(s["p_kb"], 1 if first else b * 4 + 2)
                    if not first:
                        pe.wait_ge(s["v_qTl"], b * 2)
                else:
                    pe.wait_ge(s["v_min"], b * 4 + i)
                for k in range(KC):
                    for st in range(2):
                        q = slice(64 * st, 64 * st + 64)
                        if first:
                            last = T.matmul(Sb[:, st, C * k:C * k + C], qT[q, k, P * i:P * i + P],
                                            kblk[q, k, :, :].rearrange("p j n -> p (j n)"), start=True, stop=True)
                        else:
                            for n, (qq, kk) in enumerate(((qTh, kbh), (qTh, kbl), (qTl, kbh))):
                                last = T.matmul(Sb[:, st, C * k:C * k + C], qq[q, k, P * i:P * i + P],
                                                kk[q, k, :, :].rearrange("p j n -> p (j n)"), start=(n == 0), stop=(n == 2))
                last.then_inc(s["t_s"], 1)

            def probs_T(b, i, first):
                pe.wait_ge(s["a_exp"], b * 4 + i + 1)
                if i > 0:
                    pe.wait_ge(s["a_PT"], b * 8 + 2 * i)
                elif not first:
                    pe.wait_ge(s["v_x2l"], b * 2)
                for hlf in range(2):
                    for j in range(4):
                        q = 4 * hlf + j
                        last = T.transpose(A[hlf][:, P * j:P * j + P], SC[:, i % 2, P * q:P * q + P], ident[:])
                    last.then_inc(s["t_PT"], 1)

            def values(b, i, first):
                pe.wait_ge(s["a_PT"], b * 8 + 2 * i + 2)
                if i >= 2:
                    pe.wait_ge(s["v_zn"], b * 4 + i - 1)
                if i == 0 and first:
                    pe.wait_ge(s["p_kb"], 2)
                    pe.wait_ge(s["v_vb"], 2 * B)
                if i == 2 and not first:
                    pe.wait_ge(s["v_slot"], b)
                for st in range(2):
                    for k in range(KC):
                        for jj in range(2):
                            q = (st * 2 + k) * 2 + jj
                            r = 4 * k + 2 * st + jj
                            last = T.matmul(Zb[i % 2][:, ZW * r:ZW * r + ZW], PT[:, q, :], vcur[:, ZW * r:ZW * r + ZW],
                                            start=True, stop=True)
                last.then_inc(s["t_z"], 1)

            def z_T(b):
                pe.wait_ge(s["v_zn"], b * 4 + 4)
                pe.wait_ge(s["a_PT"], b * 8 + 8)
                for k in range(KC):
                    for i in range(TB):
                        last = T.transpose(A[k][:, P * i:P * i + P], Zn[:, i, P * k:P * k + P], ident[:])
                    last.then_inc(s["t_ZT"], 1)

            def project_out(b, first):
                pe.wait_ge(s["a_ZT"], b * 2 + 2)
                if not first:
                    pe.wait_ge(s["v_ZTl"], b * 2)
                for h in range(2):
                    for j in range(2):
                        i = 2 * h + j
                        n = 0
                        for z, w in (((ZT, wo),) if first else ((ZTh, woh), (ZTh, wol), (ZTl, woh))):
                            for k in range(KC):
                                last = T.matmul(A[h][:, C * j:C * j + C], z[:, k, P * i:P * i + P], w[:, k, :],
                                                start=(n == 0), stop=(n == (1 if first else 3) * KC - 1))
                                n += 1
                    last.then_inc(s["t_wo"], 1)

            def rank(f, normalised):
                pe.wait_ge(s["v_sel"], f + 1)
                pe.wait_ge(s["v_zn"], normalised)
                T.matmul(ranks[:, 0:TB + 1], tri[:], sel[:], start=True, stop=False)
                T.matmul(ranks[:, 0:TB + 1], ones[:], R[:], start=False, stop=False)
                for j in range(1, TB + 1):
                    last = T.matmul(ranks[:, j:TB + 1], ones[:], sel[:, 0:TB + 1 - j], start=False, stop=(j == TB))
                last.then_inc(s["t_rank"], 1)

            def ffn_in_T(src):
                for k in range(KC):
                    for i in range(TB):
                        last = T.transpose(A[k][:, P * i:P * i + P], src[:, i, P * k:P * k + P], ident[:])
                    last.then_inc(s["t_T2"], 1)

            def shared_in_T(f):
                pe.wait_ge(s["v_row"], f * 4 + 4)
                ffn_in_T(row)

            def up(f, c, at=odd_w, routed=False, width=S):
                if c == 0:
                    pe.wait_ge(s["a_x2h"], f * 2 + 2)
                if routed:
                    pe.wait_ge(s["a_hf"], f * 8 + (c - 3))
                    if c in (2, 3):
                        pe.wait_ge(s["v_y"], f * 4 + (c - 3))
                elif c >= 2:
                    pe.wait_ge(s["a_hf"], f * 8 + c - 1)
                n = 0
                for kind, xx in (("1h", x2h), ("1l", x2h), ("1h", x2l)):
                    for k in range(KC):
                        if c == 0 and xx is x2l:
                            pe.wait_ge(s["v_x2l"], f * 2 + k + 1)
                        last = T.matmul(ps[:, up_bank(c, routed), 0:width], at[kind][:, k, P * c:P * c + P], xx[:, k, 0:width],
                                        start=(n == 0), stop=(n == 3 * KC - 1))
                        n += 1
                last.then_inc(s["t_up"], 1)

            def down(f, d, at=odd_w, banks=U):
                if d == 0:
                    pe.wait_ge(s["v_hl"], f * 8 + 7)
                if len(banks) == 4:
                    if d < 2:
                        pe.wait_ge(s["v_y"], f * 4 + (d - 3))
                    else:
                        pe.wait_ge(s["a_hf"], f * 8 + 5 + d)
                elif d >= 2:
                    pe.wait_ge(s["v_y"], f * 4 + (d - 1))
                else:
                    pe.wait_ge(s["a_hf"], f * 8 + 7 + d)
                n = 0
                for c in range(HC):
                    if d == 0 and c == HC - 1:
                        pe.wait_ge(s["v_hl"], f * 8 + 8)
                    for hid, kind in ((hh, "2h"), (hh, "2l"), (hl, "2h")):
                        last = T.matmul(banks[d % len(banks)][:, 0:C], hid[:, c, P * d:P * d + P], at[kind][:, c, :],
                                        start=(n == 0), stop=(n == 3 * HC - 1))
                        n += 1
                last.then_inc(s["t_down"], 1)

            def context_values(pair):
                if pair == 0:
                    pe.wait_ge(s["d_wv"], 16)
                    pe.wait_ge(s["a_ctxT"], 2)
                if pair == 2:
                    pe.wait_ge(s["v_kT"], 2)
                for b in (2 * pair, 2 * pair + 1):
                    for k in range(KC):
                        last = T.matmul((U + Zb)[pair][:, (b % 2) * C:(b % 2) * C + C], ctxT2[:, k, b, :, :].rearrange("p d n -> p (d n)"),
                                        wv[:, k, :], start=(k == 0), stop=(k == KC - 1))
                last.then_inc(s["t_v"], 1)

            def with_relu_b1(e, first_c, end_c):
                if e == 0 and first_c == 0:
                    pe.wait_ge(s["d_w2e"], 16)
                    pe.wait_ge(s["a_rbc"], 2)
                    pe.wait_ge(s["v_vb"], B)
                for c in range(first_c, end_c):
                    last = T.matmul(U[e][:, 0:C], rbc[e][:, c, :], w2e[:, e, c, :], start=(c == 0), stop=(c == HC - 1))
                if end_c == HC:
                    last.then_inc(s["t_const"], 1)

            def attention(b, first, last):
                f = b - 1
                if first:
                    context_values(0)
                    project_q_whole()
                    context_values(1)
                    scores(0, 0, True)
                    context_values(2)
                else:
                    shared_in_T(f)
                scores(b, 1, first)
                if first:
                    context_values(3)
                    with_relu_b1(0, 0, 4)
                else:
                    up(f, 0)
                    up(f, 1)
                    up(f, 2)
                probs_T(b, 0, first)
                scores(b, 2, first)
                if first:
                    with_relu_b1(0, 4, HC)
                else:
                    up(f, 3)
                values(b, 0, first)
                probs_T(b, 1, first)
                scores(b, 3, first)
                if first:
                    with_relu_b1(1, 0, 2)
                else:
                    up(f, 4)
                    up(f, 5)
                    rank(f, b * 4 + 1)
                values(b, 1, first)
                probs_T(b, 2, first)
                if first:
                    with_relu_b1(1, 2, 4)
                else:
                    up(f, 6)
                values(b, 2, first)
                probs_T(b, 3, first)
                if first:
                    with_relu_b1(1, 4, 6)
                    values(0, 3, True)
                    transposed_queries(1)
                    z_T(0)
                    with_relu_b1(1, 6, HC)
                    pe.wait_ge(s["d_wo"], 16)
                    project_out(0, True)
                    pe.wait_ge(s["v_wqo"], 1)
                    project_q(1)
                    scores(1, 0, False)
                else:
                    up(f, 7)
                    values(b, 3, False)
                    down(f, 0)
                    z_T(b)
                    down(f, 1)
                    if not last:
                        transposed_queries(b + 1)
                    project_out(b, False)
                    if not last:
                        project_q(b + 1)
                    down(f, 2)
                    if not last:
                        scores(b + 1, 0, False)
                    down(f, 3)

            pe.wait_ge(s["p_ident"], 4)
            pe.wait_ge(s["d_ctx"], 16)
            for k in range(KC):
                for j in range(TB):
                    last = T.transpose(A[k][:, P * j:P * j + P], ctx_nat[:, j, P * k:P * k + P], ident[:])
                last.then_inc(s["t_ctx"], 1)
            pe.wait_ge(s["d_wk"], 16)
            for k in range(KC):
                pe.wait_ge(s["v_ctxT"], k + 1)
                for m in range(KC):
                    last = T.matmul(Zb[m].rearrange("p (b n) -> p b n", n=KEYS), wk[:, k, P * m:P * m + P], ctxT2[:, k, :, 0, :],
                                    start=(k == 0), stop=(k == KC - 1))
                    if k == KC - 1:
                        last.then_inc(s["t_k"], 1)
            transposed_queries(0, True)
            pe.wait_ge(s["d_wq"], 16)
            attention(0, True, False)
            pe.wait_ge(s["p_wl"], 2)
            pe.wait_ge(s["v_crow"], 2)
            pe.wait_ge(s["v_wqo"], 2)
            with pe.Fori(1, B - 1) as b:
                attention(b, False, False)
            attention(B - 1, False, True)
            f = B - 1
            shared_in_T(f)
            pe.wait_ge(s["v_y"], f * 4)
            for c in range(HC):
                up(f, c)
                if c == 2:
                    rank(f, B * TB)
            for d in range(TB):
                down(f, d)
                if d == 1:
                    pe.wait_ge(s["d_xg"], 16)
                    ffn_in_T(xg)

            def routed(t, at, last):
                f = t + B
                pe.wait_ge(s["v_w1l"], t + 1)
                for c in range(HC):
                    up(f, c, at, True, HALF if last else S)
                if not last:
                    pe.wait_ge(s["d_xg"], t * 16 + 32)
                    pe.wait_ge(s["v_x2l"], f * 2 + 2)
                    ffn_in_T(xg)
                pe.wait_ge(s["v_w2l"], t + 1)
                for d in range(TB // 2 if last else TB):
                    down(f, d, at, routed_down)

            with pe.Fori(0, ROUTED // 2) as u:
                routed(u * 2, even_w, False)
                routed(u * 2 + 1, odd_w, False)
            routed(ROUTED - 1, even_w, True)


_INS = ["x", "ctx_1024", "mask_Bx1xSxS2_ik1",
        "L0_xattn_WQ", "L0_xattn_bQ", "L0_xattn_WK", "L0_xattn_bK", "L0_xattn_WV", "L0_xattn_bV", "L0_xattn_WO", "L0_xattn_bO",
        "L0_ffn_gate_w", "L0_ffn_w1", "L0_ffn_b1", "L0_ffn_w2", "L0_ffn_b2", "L0_ffn_sw1", "L0_ffn_sb1", "L0_ffn_sw2", "L0_ffn_sb2"]
_OUTS = [((8, 512, 256), "float32")]


def _laid_out(name, a):
    short = name.split("_", 2)[-1]
    if short in ("WQ", "WK", "WV", "WO", "sw1", "sw2"):
        return a.reshape(-1, P, a.shape[1]).transpose(1, 0, 2)
    if short in ("w1", "w2"):
        return a.reshape(a.shape[0], -1, P, a.shape[2]).transpose(0, 2, 1, 3)
    if short in ("bQ", "bK", "sb1"):
        return a.reshape(-1, P).T
    if short == "b1":
        return a.reshape(a.shape[0], -1, P).transpose(2, 0, 1)
    return a


def kernel(**inputs):
    import numpy as _np
    import concourse.bacc as _bacc
    from concourse import mybir as _mybir
    from concourse.bass_utils import run_bass_kernel_spmd as _run

    nc = _bacc.Bacc("TRN2", target_bir_lowering=False, num_devices=1)
    arrays, args = {}, []
    for name in _INS:
        a = _np.ascontiguousarray(_laid_out(name, _np.asarray(inputs[name])))
        arrays[f"in_{name}_dram"] = a
        args.append(nc.dram_tensor(f"in_{name}_dram", a.shape, _mybir.dt.from_np(a.dtype), kind="ExternalInput").ap())
    for i, (shape, dtype) in enumerate(_OUTS):
        dt = _mybir.dt.from_np(_np.dtype(dtype))
        args.append(nc.dram_tensor(f"out_{i}_dram", shape, dt, kind="ExternalOutput").ap())
    attention_and_routed_ffn(nc, *args)
    r = _run(nc, [arrays], core_ids=[0])
    got = tuple(r.results[0][f"out_{i}_dram"] for i in range(len(_OUTS)))
    return got[0]
```
